# Optimizing a Trainium2 kernel written in Bass

```python
import numpy as np
import jax
import jax.numpy as jnp

def _softmax(x, axis=-1):
    return jax.nn.softmax(x, axis=axis)

def _gelu(x):
    return jax.nn.gelu(x, approximate=True)

def _silu(x):
    return jax.nn.silu(x)

def _sigmoid(x):
    return jax.nn.sigmoid(x)

def _layernorm(x, axis=-1, eps=1e-05):
    m = jnp.mean(x, axis=axis, keepdims=True)
    v = jnp.var(x, axis=axis, keepdims=True)
    return (x - m) / jnp.sqrt(v + eps)

def _scatter_add(tgt, idx, src, axis=0):
    return tgt.at[idx].add(src)

def _segment_sum(src, seg, n):
    return jax.ops.segment_sum(src, seg, n)
kernel_name = 'mk_adj_ffn_d1_adj_r2_f661e4'

def setup_inputs(seed: int=0):
    np.random.seed(seed)
    _w = jnp.asarray

    def _rec_inputs():
        import jax
        import jax.numpy as jnp
        _gk = jax.random.key(seed)
        x = -0.0003929 + 0.9999 * jax.random.normal(jax.random.fold_in(_gk, 1), (32, 256, 512), jnp.float32)
        _w = (1.0 + jnp.arange(256, dtype=jnp.float32)) ** (-0.5)
        _w = _w / _w.mean()
        _pij = jnp.clip(0.0078125 * _w[:, None] * _w[None, :], 0.0, 1.0)
        _a = jax.random.uniform(jax.random.fold_in(_gk, 2), (256, 256)) < _pij
        _a = jnp.logical_or(_a, jnp.swapaxes(_a, -1, -2))
        _a = jnp.logical_or(_a, jnp.eye(256, dtype=bool))
        _af = _a.astype(jnp.float32)
        _af = _af * jax.random.uniform(jax.random.fold_in(_gk, 3), (256, 256), jnp.float32, 0.05, 0.198159)
        adj = _af
        return (x, adj)
    x, adj = _rec_inputs()

    def _L0_gnn_setup():
        import jax, jax.numpy as jnp
        import numpy as np
        NEG_SLOPE = 0.01
        key = jax.random.key(seed)
        k1, k2, k3, k4, k5 = jax.random.split(key, 5)
        B, C, N, O = (32, 256, 512, 256)
        x = jax.random.normal(k1, (B, C, N), dtype=jnp.float32)
        wq = jax.random.normal(k2, (C,), dtype=jnp.float32) * (1.0 / np.sqrt(C))
        wk = jax.random.normal(k3, (C,), dtype=jnp.float32) * (1.0 / np.sqrt(C))
        wm = jax.random.normal(k4, (O, C), dtype=jnp.float32) * (1.0 / np.sqrt(C))
        bm = jax.random.normal(k5, (O,), dtype=jnp.float32) * 0.01
        return {'x': x, 'wq': wq, 'wk': wk, 'wm': wm, 'bm': bm}
    _L0_gnn_all = _L0_gnn_setup()
    _L0_gnn_in = {k: v for k, v in _L0_gnn_all.items() if k in ('wq', 'wk', 'bm')}
    del _L0_gnn_all

    def _L0_ffn_setup():
        import jax, jax.numpy as jnp
        import numpy as np
        B, T, C = (8, 1024, 512)
        E, K = (8, 2)
        H = 4 * C
        CAP_FACTOR = 1.2
        EPS = 1e-09
        key = jax.random.key(seed)
        ks = jax.random.split(key, 6)
        x = jax.random.normal(ks[0], (B, T, C), dtype=jnp.float32)
        router_w = jax.random.normal(ks[1], (E, C), dtype=jnp.float32) * 0.02
        router_b = jnp.zeros((E,), dtype=jnp.float32)
        fc1_w = jax.random.normal(ks[2], (E, H, C), dtype=jnp.float32) * (1.0 / np.sqrt(C))
        fc1_b = jnp.zeros((E, H), dtype=jnp.float32)
        fc2_w = jax.random.normal(ks[3], (E, C, H), dtype=jnp.float32) * (1.0 / np.sqrt(H))
        fc2_b = jnp.zeros((E, C), dtype=jnp.float32)
        layer_scale = jnp.full((E, C), 0.1, dtype=jnp.float32)
        return {'x': x, 'router_w': router_w, 'router_b': router_b, 'fc1_w': fc1_w, 'fc1_b': fc1_b, 'fc2_w': fc2_w, 'fc2_b': fc2_b, 'layer_scale': layer_scale}
    _L0_ffn_all = _L0_ffn_setup()
    _L0_ffn_in = {k: v for k, v in _L0_ffn_all.items() if k in ('router_w', 'router_b', 'fc1_w', 'fc1_b', 'fc2_w', 'fc2_b', 'layer_scale')}
    del _L0_ffn_all
    return {'x': x, 'adj': adj, 'L0_gnn_wq': _L0_gnn_in['wq'], 'L0_gnn_wk': _L0_gnn_in['wk'], 'L0_gnn_bm': _L0_gnn_in['bm'], 'L0_ffn_router_w': _L0_ffn_in['router_w'], 'L0_ffn_router_b': _L0_ffn_in['router_b'], 'L0_ffn_fc1_w': _L0_ffn_in['fc1_w'], 'L0_ffn_fc1_b': _L0_ffn_in['fc1_b'], 'L0_ffn_fc2_w': _L0_ffn_in['fc2_w'], 'L0_ffn_fc2_b': _L0_ffn_in['fc2_b'], 'L0_ffn_layer_scale': _L0_ffn_in['layer_scale']}

def reference(x, adj, L0_gnn_wq, L0_gnn_wk, L0_gnn_bm, L0_ffn_router_w, L0_ffn_router_b, L0_ffn_fc1_w, L0_ffn_fc1_b, L0_ffn_fc2_w, L0_ffn_fc2_b, L0_ffn_layer_scale):
    import jax
    import jax.numpy as jnp

    def _L0_gnn_ref(x, wq, wk, wm, bm):
        import jax, jax.numpy as jnp
        import numpy as np
        NEG_SLOPE = 0.01
        q = jnp.einsum('c,bcn->bn', wq, x)
        k = jnp.einsum('c,bcn->bn', wk, x)
        scores = q[:, None, :] + k[:, :, None]
        scores = jnp.where(scores > 0, scores, NEG_SLOPE * scores)
        att = jax.nn.softmax(scores, axis=-1)
        agg = jnp.einsum('bcn,bmn->bcm', x, att)
        out = jnp.einsum('oc,bcm->bom', wm, agg) + bm[None, :, None]
        return jax.nn.relu(out)

    def _L0_ffn_ref(x, router_w, router_b, fc1_w, fc1_b, fc2_w, fc2_b, layer_scale):
        import jax, jax.numpy as jnp
        import numpy as np
        B, T, C = (8, 1024, 512)
        E, K = (8, 2)
        H = 4 * C
        CAP_FACTOR = 1.2
        EPS = 1e-09
        Bb, Tt, Cc = x.shape
        N = Bb * Tt
        KN = K * N
        capacity = int(CAP_FACTOR * (N // E + 1))
        xf = x.reshape(N, Cc)
        logits = xf @ router_w.T + router_b
        probs = jax.nn.softmax(logits, axis=-1)
        top_vals, top_inds = jax.lax.top_k(probs, K)
        top_vals = top_vals / (jnp.sum(top_vals, axis=-1, keepdims=True) + EPS)
        e_flat = top_inds.T.reshape(-1)
        w_flat = top_vals.T.reshape(-1)
        valid = w_flat > EPS
        onehot = (e_flat[:, None] == jnp.arange(E)[None, :]) & valid[:, None]
        pos = jnp.cumsum(onehot.astype(jnp.int32), axis=0) - 1
        pos_own = jnp.take_along_axis(pos, e_flat[:, None], axis=1)[:, 0]
        keep = valid & (pos_own < capacity)
        scores = jnp.where(keep[None, :] & (e_flat[None, :] == jnp.arange(E)[:, None]), jnp.arange(KN)[None, :], KN)
        sel = jnp.sort(scores, axis=1)[:, :capacity]
        slot_valid = sel < KN
        sel_c = jnp.where(slot_valid, sel, 0)
        tok = sel_c % N
        wgt = jnp.where(slot_valid, w_flat[sel_c], 0.0)
        toks = xf[tok]
        h = jax.nn.gelu(jnp.einsum('etc,ehc->eth', toks, fc1_w) + fc1_b[:, None, :], approximate=False)
        y = jnp.einsum('eth,ech->etc', h, fc2_w) + fc2_b[:, None, :]
        y = toks + y * layer_scale[:, None, :]
        out = jnp.zeros((N, Cc), dtype=x.dtype)
        out = out.at[tok.reshape(-1)].add((wgt[..., None] * y).reshape(-1, Cc))
        return out.reshape(Bb, Tt, Cc)
    x = x + _L0_gnn_ref(_layernorm(x, axis=-1), L0_gnn_wq, L0_gnn_wk, adj, L0_gnn_bm)
    x = x + _L0_ffn_ref(_layernorm(x, axis=-1), L0_ffn_router_w, L0_ffn_router_b, L0_ffn_fc1_w, L0_ffn_fc1_b, L0_ffn_fc2_w, L0_ffn_fc2_b, L0_ffn_layer_scale)
    return x

_drawn_inputs = setup_inputs


def setup_inputs(seed=0):
    import zlib

    import numpy as np

    out = dict(_drawn_inputs(seed))
    spreads = {'L0_ffn_router_b': (0.0, 0.1),
     'L0_ffn_fc1_b': (0.0, 2.0),
     'L0_ffn_fc2_b': (0.0, 0.8),
     'L0_ffn_layer_scale': (0.10000000149011612, 0.6)}
    factors = {'adj': 4.193, 'L0_gnn_wq': 3.788, 'L0_gnn_wk': 4.131, 'L0_gnn_bm': 5.756}
    for name, (base, spread) in spreads.items():
        noise = np.random.default_rng([zlib.crc32(name.encode()), seed]).standard_normal(out[name].shape)
        drawn = base * np.exp(spread * noise) if base else spread * noise
        out[name] = jnp.asarray(drawn.astype(out[name].dtype))
    for name, factor in factors.items():
        out[name] = (out[name] * factor).astype(out[name].dtype)
    return out
```

```python
from contextlib import ExitStack

import concourse.bass as bass
from concourse import mybir

ALU = mybir.AluOpType
ACT = mybir.ActivationFunctionType
AX = mybir.AxisListType
F32 = mybir.dt.float32
F32R = mybir.dt.float32r
I32 = mybir.dt.int32
U32 = mybir.dt.uint32

P = 128
B, C, N = 32, 256, 512
CT = C // P
KC = N // P
E, H = 8, 2048
TOKENS = B * C
CAP = int(1.2 * (TOKENS // E + 1))
TT = 5
TM = CAP // (2 * TT)
HALF = TT * TM
HP = HALF + HALF % 2
NH = HP // 2
MC = H // P
S1 = 9472
S2 = TOKENS
TAB2 = E * S1
ROWS = TAB2 + E * S2
BIG = 1 << 22
EPS_LN = 1e-5
EPS_W = 1e-9
SLOPE = 0.01
RING_X = 4
RING_W = 4
PASSES = 2 * E
INIT_OPS = 17
assert S1 >= TOKENS + CAP and HALF * 2 == CAP


def wait(eng, sem, value):
    if isinstance(value, int) and value <= 0:
        return
    eng.wait_ge(sem, value)


def wait_apart(eng, apart, sem, value):
    wait(eng, sem, value)
    eng.sem_inc(apart, 1)


class Chain:

    def __init__(self, eng, sem, per, rnd):
        self.eng, self.sem, self.per, self.base, self.n = eng, sem, per, per * rnd, 0

    def __call__(self, ins, apart=None):
        ins.then_inc(self.sem, 1)
        self.n += 1
        if apart is None:
            self.eng.wait_ge(self.sem, self.base + self.n)
        else:
            wait_apart(self.eng, apart, self.sem, self.base + self.n)

    def end(self):
        assert self.n == self.per, (self.n, self.per)


def gnn_moe_kernel(nc, x, adj_t, wq, wk, bm, router_wt, router_b, w_cat, fc1_b, fc2_b, scale, out):
    xn_dram = nc.dram_tensor("xn_rows", (TOKENS, N), F32).ap()
    table = nc.dram_tensor("slot_table", (ROWS, 2), I32).ap()

    with ExitStack() as ctx:
        def sb(name, shape, dt=F32):
            return ctx.enter_context(nc.sbuf_tensor(name, shape, dt))

        def psum(name, shape):
            return ctx.enter_context(nc.psum_tensor(name, shape, F32))

        def sem(name):
            return ctx.enter_context(nc.semaphore(name))

        ident = sb("ident", [P, P])
        lower = sb("lower", [P, P])
        ones = sb("ones", [P, P])
        iota8 = sb("iota8", [P, E])
        stride_k = sb("stride_k", [P, 2 * CT])
        base_k = sb("base_k", [P, 2 * CT])
        tok_f = sb("tok_f", [P, CT])
        adj_sb = sb("adj_sb", [P, CT, C])
        wq_sb = sb("wq_sb", [P, CT])
        wk_sb = sb("wk_sb", [P, CT])
        wk_rep = sb("wk_rep", [P, CT, P])
        bm_sb = sb("bm_sb", [P, CT])
        rw_sb = sb("rw_sb", [P, KC, E])
        rb_sb = sb("rb_sb", [P, CT, E])
        b1_sb = sb("b1_sb", [P, E * MC])

        X = sb("X", [P, RING_X, CT, N])
        xn = sb("xn", [P, 2, CT, N])
        yT = sb("yT", [P, 2, KC, C])
        uv = sb("uv", [P, 2, N])
        fB = sb("fB", [P, 2, N])
        fD = sb("fD", [P, 2, N])
        asum = sb("asum", [P, N])
        rden = sb("rden", [P, N])
        x2 = sb("x2", [P, 2, CT, N])
        st1 = sb("st1", [P, CT, 6])
        mv1 = sb("mv1", [P, 2, CT, 2])
        ve1 = sb("ve1", [P, CT])
        rs1 = sb("rs1", [P, 2, CT])
        st2 = sb("st2", [P, CT, 6])
        mv2 = sb("mv2", [P, CT, 2])
        ve2 = sb("ve2", [P, CT])
        rs2 = sb("rs2", [P, CT])
        mhalf = sb("mhalf", [P, CT])
        qs = sb("qs", [P, 2, KC])
        qr = sb("qr", [P, 1])
        qm = sb("qm", [P, 1])
        nq = sb("nq", [P, 2])
        fA = sb("fA", [P, 2, KC])
        fC = sb("fC", [P, 2, KC])
        lg = sb("lg", [P, CT, E])
        m8 = sb("m8", [P, CT, 8])
        i8 = sb("i8", [P, CT, 8], U32)
        nm = sb("nm", [P, CT])
        ex = sb("ex", [P, CT, 8])
        Z = sb("Z", [P, CT])
        zz = sb("zz", [P, CT])
        zr = sb("zr", [P, CT])
        i2 = sb("i2", [P, CT, 2])
        w2 = sb("w2", [P, CT, 2])
        ok = sb("ok", [P, CT, 2])
        onehot = sb("onehot", [P, CT, 2 * E])
        seen = sb("seen", [P, 2 * E])
        prod = sb("prod", [P, 2 * CT, E])
        pos = sb("pos", [P, 2 * CT])
        dst = sb("dst", [P, 2 * CT])
        dst_i = sb("dst_i", [P, 2, 2 * CT], U32)
        pay = sb("pay", [P, 2, 2 * CT, 2], I32)
        cnt = sb("cnt", [P, E], I32)

        w_raw = sb("w_raw", [P, 2, 2 * N])
        w_hi = sb("w_hi", [P, RING_W, 2 * N], F32R)
        w_lo = sb("w_lo", [P, RING_W, 2 * N], F32R)
        t_hi = sb("t_hi", [P, 2, KC, HP], F32R)
        t_lo = sb("t_lo", [P, 2, KC, HP], F32R)
        h_raw = sb("h_raw", [P, 2, NH])
        h_hi = sb("h_hi", [P, 2, HP], F32R)
        h_lo = sb("h_lo", [P, 2, HP], F32R)
        rows = sb("rows", [P, 2, TT, N])
        yo = sb("yo", [P, TT, N])
        b2_sb = sb("b2_sb", [P, 2, N])
        ls_sb = sb("ls_sb", [P, 2, N])
        slots = sb("slots", [P, 2, TT, 2], I32)

        flat = rows[:, :, :, :].rearrange("p a t n -> p (a t n)")
        tq = flat[:, 0:KC * N].rearrange("p (k n) -> p k n", k=KC)
        att = flat[:, KC * N:2 * KC * N].rearrange("p (k n) -> p k n", k=KC)
        yflat = yo[:, :, :].rearrange("p t n -> p (t n)")
        z = yflat[:, 0:CT * N].rearrange("p (c n) -> p c n", c=CT)
        xT = yflat[:, CT * N:2 * CT * N].rearrange("p (j k t) -> p j k t", j=CT, k=KC)
        xn2 = sb("xn2", [P, CT, N])
        empty = flat[0:E, 0:2 * CAP].bitcast(I32)

        bank = [psum(f"bank{i}", [P, N]) for i in range(8)]
        KB = bank[0]
        Y = [bank[1], bank[2]]
        AG = [bank[3], bank[4]]
        DEN = bank[5]
        TP = bank[6]
        SM = bank[7]
        q_ps = SM[:, 0:KC]
        lg_ps = SM[:, 16:16 + CT * E].rearrange("p (j e) -> p j e", j=CT)
        rank_ps = SM[:, 32:32 + CT * 2 * E]
        cnt_ps = SM[:, 64:64 + E]
        YB = bank[0:TT]
        HB = bank[TT:TT + 2]
        TB = bank[7]

        ld_const = sem("ld_const")
        ld_x = [sem(f"ld_x{i}") for i in range(RING_X)]
        st_x2 = [sem(f"st_x2{i}") for i in range(2)]
        st_xn = sem("st_xn")
        st_empty = sem("st_empty")
        sc_tab = [sem(f"sc_tab{i}") for i in range(2)]
        cp_tab = sem("cp_tab")
        ld_w = [sem(f"ld_w{i}") for i in range(2)]
        ld_slots = [sem(f"ld_slots{i}") for i in range(2)]
        ld_b2 = [sem(f"ld_b2{i}") for i in range(2)]
        ga = [sem(f"ga{i}") for i in range(2)]
        sc_out = sem("sc_out")
        c_pool = sem("c_pool")
        apart = sem("apart")
        empty_ok = sem("empty_ok")
        pow1 = sem("pow1")
        pow2 = sem("pow2")
        qmax = sem("qmax")
        asum_ok = sem("asum_ok")
        pool_sum = sem("pool_sum")
        x2_ok = sem("x2_ok")
        pool_y = sem("pool_y")
        y_res = sem("y_res")
        c_dve = sem("c_dve")
        var1 = sem("var1")
        s_st1 = sem("s_st1")
        xn_ok = sem("xn_ok")
        q_read = sem("q_read")
        q_red = sem("q_red")
        uv_ok = sem("uv_ok")
        att_ok = sem("att_ok")
        rden_ok = sem("rden_ok")
        z_ok = sem("z_ok")
        s_st2 = sem("s_st2")
        var2 = sem("var2")
        xn2_ok = sem("xn2_ok")
        s_ra = sem("s_ra")
        s_ra2 = sem("s_ra2")
        oh_ok = sem("oh_ok")
        ra_ok = sem("ra_ok")
        s_rb = sem("s_rb")
        route_ok = sem("route_ok")
        cnt_ok = sem("cnt_ok")
        w_ready = sem("w_ready")
        tok_hi = sem("tok_hi")
        tok_ready = sem("tok_ready")
        h_hi_ok = sem("h_hi_ok")
        h_ready = sem("h_ready")
        y_read = sem("y_read")
        y_scaled = sem("y_scaled")
        tq_ok = sem("tq_ok")
        yT_ok = sem("yT_ok")
        fac_ok = sem("fac_ok")
        relu_ok = sem("relu_ok")
        xT_ok = sem("xT_ok")
        ex_ok = sem("ex_ok")
        w_hi_ok = sem("w_hi_ok")
        gelu_ok = sem("gelu_ok")
        kb_mm = sem("kb_mm")
        q_mm = sem("q_mm")
        y_mm = sem("y_mm")
        rank_mm = sem("rank_mm")
        ag_mm = sem("ag_mm")
        den_mm = sem("den_mm")
        t_mm = sem("t_mm")
        lg_mm = sem("lg_mm")
        cnt_mm = sem("cnt_mm")
        tok_mm = sem("tok_mm")
        fc1_mm = sem("fc1_mm")
        fc2_mm = sem("fc2_mm")

        FIRST, LAST = 6, 30
        STEPS = B + 3

        def steps(eng, step):
            for s in range(-1, FIRST):
                step(s, s % 4)
            with eng.Fori(0, (LAST - FIRST) // 4) as j:
                for u in range(4):
                    step(4 * j + (FIRST + u), (FIRST + u) % 4)
            for s in range(LAST, STEPS):
                step(s, s % 4)

        def live(b):
            return not isinstance(b, int) or 0 <= b < B

        def experts(eng, expert):
            expert(0, True, False)
            with eng.Fori(1, E - 1) as e:
                expert(e, False, False)
            expert(E - 1, False, True)

        block = ctx.enter_context(nc.Block())

        @block.sync
        def _(sp):
            consts = [
                (adj_sb[:, :, :], adj_t.rearrange("(k p) o -> p k o", p=P)),
                (wq_sb[:, :], wq.rearrange("(k p) -> p k", p=P)),
                (wk_sb[:, :], wk.rearrange("(k p) -> p k", p=P)),
                (bm_sb[:, :], bm.rearrange("(k p) -> p k", p=P)),
                (rw_sb[:, :, :], router_wt.rearrange("(k p) e -> p k e", p=P)),
                (rb_sb[:, 0, :], router_b.rearrange("(a e) -> a e", a=1).to_broadcast([P, E])),
                (rb_sb[:, 1, :], router_b.rearrange("(a e) -> a e", a=1).to_broadcast([P, E])),
                (b1_sb[:, :], fc1_b),
            ]

            def load_x(b, r):
                wait_apart(sp, apart, x2_ok, b - (RING_X - 1))
                sp.dma_start(X[:, r, :, :], x[b].rearrange("(c p) n -> p c n", p=P)).then_inc(ld_x[r], 16)

            load_x(0, 0)
            with nc.allow_non_contiguous_dma(reason="small constants"):
                for dst_ap, src_ap in consts:
                    sp.dma_start(dst_ap, src_ap).then_inc(ld_const, 16)
            load_x(1, 1)
            sp.wait_ge(empty_ok, 1)
            for part, stride in ((0, S1), (TAB2, S2)):
                to = table[part:part + E * stride, :].rearrange("(e s) w -> e (s w)", e=E)[:, 0:2 * CAP]
                sp.dma_start(to, empty).then_inc(st_empty, 16)
            for k in range(2):
                sp.dma_start(w_raw[:, k, :], w_cat[0, k]).then_inc(ld_w[k], 16)

            out_b = out.rearrange("b (c p) n -> b p c n", p=P)
            xn_b = xn_dram.rearrange("(b c p) n -> b p c n", c=CT, p=P)

            def step(s, r):
                if live(s + 2) and not (isinstance(s, int) and s < 0):
                    load_x(s + 2, (r + 2) % 4)
                if live(s - 2):
                    wait_apart(sp, apart, xn2_ok, s - 1)
                    sp.dma_start(xn_b[s - 2], xn2[:, :, :]).then_inc(st_xn, 16)
                if live(s - 1):
                    wait_apart(sp, apart, x2_ok, s)
                    sp.dma_start(out_b[s - 1], x2[:, (r + 1) % 2, :, :]).then_inc(st_x2[(r + 1) % 2], 16)

            steps(sp, step)

            for i in range(2):
                sp.wait_ge(sc_tab[i], 16 * 2 * CT * B // 2)
            sp.wait_ge(cnt_ok, 1)
            for e in range(E):
                with sp.register(f"first_choices{e}") as reg:
                    sp.reg_load(reg, cnt[0:1, e:e + 1])
                    n1 = sp.snap(reg, min_val=0, max_val=TOKENS)
                    sp.dma_start(table[bass.ds(n1 + e * S1, CAP), :],
                                 table[TAB2 + e * S2:TAB2 + e * S2 + CAP, :]).then_inc(cp_tab, 16)
            sp.wait_ge(cp_tab, 16 * E)
            sp.wait_ge(st_xn, 16 * B)
            for i in range(2):
                sp.wait_ge(st_x2[i], 16 * B // 2)

            def load_pass(e, half):
                i = 2 * e + half
                wait_apart(sp, apart, y_scaled, TT * (i - 1))
                wait_apart(sp, apart, sc_out, 16 * TT * (i - 1))
                base = e * S1 + half * HALF
                sp.dma_start(slots[0:TM, half, :, :],
                             table[bass.ds(base, HALF), :].rearrange("(p t) w -> p t w", t=TT))\
                    .then_inc(ld_slots[half], 16)
                for dst_ap, src_ap in ((b2_sb, fc2_b), (ls_sb, scale)):
                    sp.dma_start(dst_ap[:, half, :], src_ap[bass.ds(e, 1), :].to_broadcast([P, N]))\
                        .then_inc(ld_b2[half], 16)

            def load_w(i_next, e, m, par):
                wait_apart(sp, apart, w_ready, i_next - 1)
                sp.dma_start(w_raw[:, par, :], w_cat[e, m]).then_inc(ld_w[par], 16)

            load_pass(0, 0)
            load_pass(0, 1)

            def expert(e, first, last):
                for half in range(2):
                    i = 2 * e + half
                    for m in range(2, 8):
                        load_w(16 * i + m, e, m, m % 2)
                    if not (first and half == 0 or last and half == 1):
                        load_pass(e + half, 1 - half)
                    with sp.Fori(4, MC // 2) as g:
                        for u in range(2):
                            load_w(16 * i + 2 * g + u, e, 2 * g + u, u)
                    if half == 0 or not last:
                        for u in range(2):
                            load_w(16 * i + (MC + u), e + half, u, u)

            experts(sp, expert)
            sp.wait_ge(sc_out, 16 * TT * PASSES)

        @block.gpsimd
        def _(pool):
            pc = Chain(pool, c_pool, INIT_OPS, 0)
            pc(pool.memset(flat, 0.0))
            pc(pool.memset(flat[0:E, 0:2 * CAP].bitcast(I32).rearrange("p (s w) -> p s w", w=2)[:, :, 0:1], BIG))
            pool.memset(ones[:, :], 1.0).then_inc(empty_ok, 1)
            pc(pool.memset(ident[:, :], 0.0))
            pc(pool.affine_select(out=ident[:, :], in_=ident[:, :], compare_op=ALU.not_equal, fill=1.0,
                                  base=0, pattern=[[-1, P]], channel_multiplier=1))
            pc(pool.memset(lower[:, :], 1.0))
            pc(pool.affine_select(out=lower[:, :], in_=lower[:, :], compare_op=ALU.is_gt, fill=0.0,
                                  base=0, pattern=[[1, P]], channel_multiplier=-1))
            pc(pool.iota(iota8[:, :], pattern=[[1, E]], base=0, channel_multiplier=0,
                         allow_small_or_imprecise_dtypes=True))
            pc(pool.iota(tok_f[:, :], pattern=[[P, CT]], base=0, channel_multiplier=1,
                         allow_small_or_imprecise_dtypes=True))
            pc(pool.memset(mhalf[:, :], -0.5))
            pc(pool.memset(seen[:, :], 0.0))
            for k, (stride, base) in enumerate(((S1, 0), (S2, TAB2))):
                pc(pool.memset(stride_k[:, k::2], float(stride)))
                pc(pool.memset(base_k[:, k::2], float(base + BIG)))
            pc(pool.memset(t_hi[:, :, :, HALF:HP].bitcast(F32), 0.0))
            pc(pool.memset(t_lo[:, :, :, HALF:HP].bitcast(F32), 0.0))
            pc(pool.memset(h_raw[:, :, :], 0.0))
            pc.end()

            def step(s, r):
                if live(s - 2):
                    wait(pool, var2, s - 1)
                    wait(pool, xn2_ok, s - 2)
                    pool.tensor_tensor(rs2[:, :], ve2[:, :], mhalf[:, :], ALU.pow).then_inc(pow2, 1)
                if live(s):
                    wait(pool, uv_ok, s)
                    wait_apart(pool, apart, q_red, s + 1)
                    pool.partition_all_reduce(qm[:, :], qr[:, :], P, bass.bass_isa.ReduceOp.max).then_inc(qmax, 1)
                if live(s - 1):
                    b = s - 1
                    pch = Chain(pool, pool_sum, 2, b)
                    wait(pool, den_mm, b)
                    wait(pool, att_ok, KC * b + 2)
                    pch(pool.tensor_tensor(asum[:, :], att[:, 0, :], att[:, 1, :], ALU.add))
                    wait(pool, att_ok, KC * b + 3)
                    pch(pool.tensor_tensor(asum[:, :], asum[:, :], att[:, 2, :], ALU.add))
                    pch.end()
                    wait(pool, att_ok, KC * b + 4)
                    pool.tensor_tensor(asum[:, :], asum[:, :], att[:, 3, :], ALU.add).then_inc(asum_ok, 1)
                if live(s - 3):
                    q = (r + 1) % 2
                    wait_apart(pool, apart, route_ok, s - 2)
                    if isinstance(s, int) and s == 3:
                        pool.wait_ge(st_empty, 32)
                    for k in range(2 * CT):
                        pool.indirect_dma_start(
                            out=table[:, :], out_offset=bass.IndirectOffsetOnAxis(ap=dst_i[:, q, k:k + 1], axis=0),
                            in_=pay[:, q, k, :], in_offset=None, bounds_check=ROWS - 1, oob_is_err=False,
                        ).then_inc(sc_tab[q], 16)
                if live(s - 1):
                    b, q = s - 1, (r + 1) % 2
                    wait(pool, relu_ok, b + 1)
                    wait(pool, st_x2[q], 8 * (b - q))
                    wait(pool, xn2_ok, b - 1)
                    pool.tensor_tensor(x2[:, q, :, :], z, X[:, (r + 3) % 4, :, :], ALU.add).then_inc(x2_ok, 1)
                if live(s + 1):
                    wait(pool, var1, s + 2)
                    pool.tensor_tensor(rs1[:, (r + 1) % 2, :], ve1[:, :], mhalf[:, :], ALU.pow).then_inc(pow1, 1)

            steps(pool, step)

            def gather(e, half):
                i = 2 * e + half
                wait_apart(pool, apart, ld_slots[half], 16 * (e + 1))
                for t in range(TT):
                    pool.indirect_dma_start(
                        out=rows[0:TM, half, t, :], out_offset=None, in_=xn_dram[:, :],
                        in_offset=bass.IndirectOffsetOnAxis(ap=slots[0:TM, half, t, 0:1].bitcast(U32), axis=0),
                        bounds_check=TOKENS - 1, oob_is_err=False,
                    ).then_inc(ga[half], 16)

            gather(0, 0)
            gather(0, 1)

            def finish(e, half):
                i = 2 * e + half
                pool.wait_ge(ld_b2[half], 32 * (e + 1))
                for t in range(TT):
                    pool.wait_ge(y_read, TT * i + (t + 1))
                    pool.tensor_tensor(yo[0:TM, t, :], yo[0:TM, t, :], ls_sb[0:TM, half, :], ALU.mult)\
                        .then_inc(pool_y, 1)
                    pool.wait_ge(pool_y, TT * i + (t + 1))
                    pool.tensor_tensor(yo[0:TM, t, :], yo[0:TM, t, :], rows[0:TM, half, t, :], ALU.add)\
                        .then_inc(y_res, 1)
                for t in range(TT):
                    pool.wait_ge(y_scaled, TT * i + (t + 1))
                    wait_apart(pool, apart, sc_out, 16 * (TT * i + t))
                    pool.indirect_dma_start(
                        out=out.rearrange("b c n -> (b c) n"),
                        out_offset=bass.IndirectOffsetOnAxis(ap=slots[0:TM, half, t, 0:1].bitcast(U32), axis=0),
                        in_=yo[0:TM, t, :], in_offset=None, bounds_check=TOKENS - 1, oob_is_err=False,
                        compute_op=ALU.add,
                    ).then_inc(sc_out, 16)

            def expert(e, first, last):
                for half in range(2):
                    finish(e, half)
                    if not last:
                        gather(e + 1, half)

            experts(pool, expert)

        @block.vector
        def _(dve):
            dve.wait_ge(c_pool, INIT_OPS)
            dve.wait_ge(ld_const, 16 * 8)
            for k in range(CT):
                dve.tensor_scalar(wk_rep[:, k, :], ones[:, :], wk_sb[:, k:k + 1], None, ALU.mult).then_inc(c_dve, 1)

            def step(s, r):
                q, q1 = r % 2, (r + 1) % 2
                if live(s):
                    wait(dve, pow1, s + 1)
                    wait(dve, y_mm, s - 1)
                    for c in range(CT):
                        ins = dve.tensor_scalar(xn[:, q, c, :], X[:, r, c, :], mv1[:, q, c, 0:1],
                                                rs1[:, q, c:c + 1], ALU.subtract, ALU.mult)
                    ins.then_inc(xn_ok, 1)
                if live(s - 3):
                    b = s - 3
                    wait(dve, ex_ok, b + 1)
                    ch = Chain(dve, s_ra2, 5, b)
                    ch(dve.scalar_tensor_tensor(out=zz[:, :], in0=Z[:, :], scalar=EPS_W, in1=ex[:, :, 1],
                                                op0=ALU.mult, op1=ALU.add))
                    ch(dve.tensor_scalar(zz[:, :], zz[:, :], 1.0, None, ALU.add))
                    ch(dve.reciprocal(zr[:, :], zz[:, :]))
                    for k in range(2):
                        ins = dve.tensor_tensor(w2[:, :, k], ex[:, :, k], zr[:, :], ALU.mult)
                    ch(ins)
                    ch(dve.tensor_scalar(ok[:, :, :], w2[:, :, :], EPS_W, None, ALU.is_gt))
                    ch.end()
                    for j in range(CT):
                        for k in range(2):
                            ins = dve.tensor_scalar(onehot[:, j, k * E:(k + 1) * E], iota8[:, :], i2[:, j, k:k + 1],
                                                    ok[:, j, k:k + 1], ALU.is_equal, ALU.mult)
                    ins.then_inc(oh_ok, 1)
                if live(s - 2):
                    b = s - 2
                    wait(dve, x2_ok, b + 1)
                    wait(dve, pow2, b)
                    ch = Chain(dve, s_st2, 2, b)
                    for c in range(CT):
                        ins = dve.bn_stats(st2[:, c, :], x2[:, q, c, :])
                    ch(ins, apart)
                    for c in range(CT):
                        ins = dve.bn_aggr(mv2[:, c, :], st2[:, c, :])
                    ch(ins)
                    ch.end()
                    dve.tensor_scalar(ve2[:, :], mv2[:, :, 1], EPS_LN, None, ALU.add).then_inc(var2, 1)
                if live(s):
                    wait(dve, q_mm, s + 1)
                    wait(dve, fac_ok, s - 1)
                    dve.tensor_copy(qs[:, q, :], q_ps).then_inc(q_read, 1)
                    dve.wait_ge(q_read, s + 1)
                    wait(dve, qmax, s)
                    dve.reduce_max(qr[:, :], qs[:, q, :], AX.X).then_inc(q_red, 1)
                if live(s - 1):
                    b = s - 1
                    wait(dve, fac_ok, b + 1)
                    wait(dve, ag_mm, b)
                    wait(dve, asum_ok, b)
                    for k in range(KC):
                        wait(dve, tq_ok, KC * b + k + 1)
                        dve.scalar_tensor_tensor(out=att[:, k, :], in0=fD[:, q1, :], scalar=fC[:, q1, k:k + 1],
                                                 in1=tq[:, k, :], op0=ALU.mult, op1=ALU.max).then_inc(att_ok, 1)
                if live(s - 3):
                    b = s - 3
                    wait(dve, rank_mm, b + 1)
                    wait(dve, sc_tab[q1], 8 * 2 * CT * (b - q1))
                    ch = Chain(dve, s_rb, 6, b)
                    oh = onehot[:, :, :].rearrange("p j (k e) -> p (j k) e", k=2)
                    ch(dve.tensor_tensor(prod[:, :, :], rank_ps.rearrange("p (a e) -> p a e", e=E), oh, ALU.mult))
                    for j in range(CT):
                        ins = dve.tensor_tensor(seen[:, :], seen[:, :], onehot[:, j, :], ALU.add)
                        if j == 0:
                            ch(ins)
                    ch(ins)
                    i2f = i2[:, :, :].rearrange("p j k -> p (j k)")
                    dve.tensor_reduce(pos[:, :], prod[:, :, :], AX.X, ALU.add)
                    ch(dve.tensor_tensor(dst[:, :], i2f, stride_k[:, :], ALU.mult))
                    ch(dve.tensor_tensor(dst[:, :], dst[:, :], pos[:, :], ALU.add))
                    ch(dve.tensor_tensor(dst[:, :], dst[:, :], base_k[:, :], ALU.add))
                    ch.end()
                    dve.scalar_tensor_tensor(out=dst_i[:, q1, :], in0=ok[:, :, :].rearrange("p j k -> p (j k)"),
                                             scalar=-float(BIG), in1=dst[:, :], op0=ALU.mult, op1=ALU.add)
                    pj = pay[:, q1, :, :].rearrange("p (j k) w -> p j k w", k=2)
                    for k in range(2):
                        dve.tensor_copy(pj[:, :, k, 0], tok_f[:, :])
                    dve.tensor_copy(pj[:, :, :, 1].bitcast(F32), w2[:, :, :]).then_inc(route_ok, 1)
                    dve.wait_ge(route_ok, b + 1)
                    dve.tensor_scalar(tok_f[:, :], tok_f[:, :], float(C), None, ALU.add).then_inc(c_dve, 1)
                    dve.wait_ge(c_dve, b + (CT + 1))
                if live(s - 2):
                    b = s - 2
                    wait(dve, pow2, b + 1)
                    wait(dve, st_xn, 16 * b)
                    wait(dve, t_mm, CT * b)
                    for c in range(CT):
                        ins = dve.tensor_scalar(xn2[:, c, :], x2[:, q, c, :], mv2[:, c, 0:1], rs2[:, c:c + 1],
                                                ALU.subtract, ALU.mult)
                    ins.then_inc(xn2_ok, 1)
                if live(s):
                    wait(dve, qmax, s + 1)
                    wait(dve, kb_mm, s + 1)
                    wait(dve, fac_ok, s)
                    dve.tensor_scalar(uv[:, 0, :], KB[:, :], qm[:, 0:1], 0.0, ALU.add, ALU.min)
                    dve.tensor_scalar(uv[:, 1, :], KB[:, :], qm[:, 0:1], 0.0, ALU.add, ALU.max)
                    dve.tensor_scalar(nq[:, 0:1], qm[:, :], -1.0, None, ALU.mult)
                    dve.tensor_scalar(nq[:, 1:2], qm[:, :], -SLOPE, None, ALU.mult).then_inc(uv_ok, 1)
                if live(s - 1):
                    b = s - 1
                    wait(dve, den_mm, b + 1)
                    dve.reciprocal(rden[:, :], DEN[:, :]).then_inc(rden_ok, 1)
                    dve.wait_ge(rden_ok, b + 1)
                    wait(dve, x2_ok, b)
                    wait(dve, ag_mm, b + 1)
                    for c in range(CT):
                        ins = dve.tensor_tensor(z[:, c, :], AG[c][:, :], rden[:, :], ALU.mult)
                    ins.then_inc(z_ok, 1)
                if live(s + 1):
                    b, rb = s + 1, (r + 1) % 4
                    dve.wait_ge(ld_x[rb], 4 * b + (16 - 4 * rb))
                    wait(dve, pow1, b)
                    ch = Chain(dve, s_st1, 2, b)
                    for c in range(CT):
                        ins = dve.bn_stats(st1[:, c, :], X[:, rb, c, :])
                    ch(ins, apart)
                    for c in range(CT):
                        ins = dve.bn_aggr(mv1[:, q1, c, :], st1[:, c, :])
                    ch(ins)
                    ch.end()
                    dve.tensor_scalar(ve1[:, :], mv1[:, q1, :, 1], EPS_LN, None, ALU.add).then_inc(var1, 1)
                if live(s - 2):
                    b = s - 2
                    wait(dve, lg_mm, b + 1)
                    wait(dve, ex_ok, b)
                    ch = Chain(dve, s_ra, 3, b)
                    ch(dve.tensor_tensor(lg[:, :, :], lg_ps, rb_sb[:, :, :], ALU.add), apart)
                    for j in range(CT):
                        ins = dve.max(m8[:, j, :], lg[:, j, :])
                    ch(ins, apart)
                    for j in range(CT):
                        ins = dve.max_index(i8[:, j, :], m8[:, j, :], lg[:, j, :])
                    ch(ins)
                    ch.end()
                    dve.tensor_copy(i2[:, :, :], i8[:, :, 0:2])
                    dve.tensor_scalar(nm[:, :], m8[:, :, 0], -1.0, None, ALU.mult).then_inc(ra_ok, 1)

            steps(dve, step)

            dve.wait_ge(cnt_mm, 1)
            dve.tensor_copy(cnt[:, :], cnt_ps).then_inc(cnt_ok, 1)

            def split_w(M, sl, par):
                dve.wait_ge(w_hi_ok, M + 1)
                dve.tensor_tensor(w_lo[:, sl, :], w_raw[:, par, :], w_hi[:, sl, :].bitcast(F32), ALU.subtract)\
                    .then_inc(w_ready, 1)

            def split_tok(i, half, t):
                dve.wait_ge(tok_mm, TT * i + (t + 1))
                src = TB[:, 0:KC * TM].rearrange("p (k t) -> p k t", k=KC)
                hi = t_hi[:, half, :, t * TM:(t + 1) * TM]
                dve.tensor_copy(hi, src).then_inc(tok_hi, 1)
                dve.wait_ge(tok_hi, TT * i + (t + 1))
                dve.tensor_tensor(t_lo[:, half, :, t * TM:(t + 1) * TM], src, hi.bitcast(F32), ALU.subtract)\
                    .then_inc(tok_ready, 1)

            def split_h(M, par):
                wait(dve, fc2_mm, M - 1)
                for n in range(2):
                    dve.wait_ge(gelu_ok, 2 * M + (n + 1))
                    hi = h_hi[:, par, n * NH:(n + 1) * NH]
                    dve.tensor_copy(hi, h_raw[:, n, :]).then_inc(h_hi_ok, 1)
                    dve.wait_ge(h_hi_ok, 2 * M + (n + 1))
                    dve.tensor_tensor(h_lo[:, par, n * NH:(n + 1) * NH], h_raw[:, n, :], hi.bitcast(F32),
                                      ALU.subtract).then_inc(h_ready, 1)

            def read_y(e, half):
                i = 2 * e + half
                dve.wait_ge(fc2_mm, 16 * i + 16)
                dve.wait_ge(ld_b2[half], 32 * (e + 1))
                wait(dve, sc_out, 16 * TT * i)
                for t in range(TT):
                    dve.tensor_tensor(yo[0:TM, t, :], YB[t][0:TM, :], b2_sb[0:TM, half, :], ALU.add)\
                        .then_inc(y_read, 1)

            def weigh_y(e, half):
                i = 2 * e + half
                for t in range(TT):
                    dve.wait_ge(y_res, TT * i + (t + 1))
                    dve.tensor_scalar(yo[0:TM, t, :], yo[0:TM, t, :], slots[0:TM, half, t, 1:2].bitcast(F32), None,
                                      ALU.mult).then_inc(y_scaled, 1)

            for M in range(3):
                split_w(M, M % RING_W, M % 2)
            for t in range(TT):
                split_tok(0, 0, t)

            def expert(e, first, last):
                for half in range(2):
                    i = 2 * e + half
                    tail = last and half == 1
                    with_prev = not (first and half == 0)
                    pe_, ph = (e, 0) if half else (e - 1, 1)

                    def round_(m, u, w=True):
                        split_h(16 * i + m, u % 2)
                        if w:
                            split_w(16 * i + m + 3, (u + 3) % RING_W, (u + 3) % 2)

                    for u in range(4):
                        if u == 1 and with_prev:
                            read_y(pe_, ph)
                        round_(u, u)
                        if u == 3 and with_prev:
                            weigh_y(pe_, ph)
                    with dve.Fori(1, 3) as g:
                        for u in range(4):
                            round_(4 * g + u, u)
                    for u in range(4):
                        m = 12 + u
                        if not tail:
                            for t in TOK_AT.get(m, ()):
                                split_tok(i + 1, 1 - half, t)
                        round_(m, u, not tail or m + 3 < MC)

            experts(dve, expert)
            read_y(E - 1, 1)
            weigh_y(E - 1, 1)

        @block.scalar
        def _(act):
            def step(s, r):
                q, q1 = r % 2, (r + 1) % 2
                if live(s - 1):
                    b = s - 1
                    act.wait_ge(fac_ok, b + 1)
                    wait(act, att_ok, KC * b)
                    for k in range(KC):
                        act.activation(tq[:, k, :], fB[:, q1, :], ACT.Copy, scale=fA[:, q1, k:k + 1])\
                            .then_inc(tq_ok, 1)
                if live(s):
                    act.wait_ge(y_mm, s + 1)
                    wait(act, ag_mm, s - 1)
                    for h in range(2):
                        ins = act.activation(yT[:, q, 2 * h:2 * h + 2, :].rearrange("p k c -> p (k c)"),
                                             Y[h][:, :], ACT.Copy)
                    ins.then_inc(yT_ok, 1)
                    act.wait_ge(uv_ok, s + 1)
                    act.activation(fA[:, q, :], qs[:, q, :], ACT.Exp, bias=nq[:, 0:1])
                    act.activation(fC[:, q, :], qs[:, q, :], ACT.Exp, bias=nq[:, 1:2], scale=SLOPE)
                    act.activation(fB[:, q, :], uv[:, 0, :], ACT.Exp, scale=1.0 - SLOPE)
                    act.activation(fD[:, q, :], uv[:, 1, :], ACT.Exp, scale=SLOPE - 1.0).then_inc(fac_ok, 1)
                if live(s - 2):
                    b = s - 2
                    act.wait_ge(t_mm, CT * b + 1)
                    wait(act, lg_mm, b)
                    act.activation(xT[:, 0, :, :].rearrange("p k t -> p (k t)"), TP[:, :], ACT.Copy).then_inc(xT_ok, 1)
                if live(s - 1):
                    act.wait_ge(z_ok, s)
                    for c in range(CT):
                        ins = act.activation(z[:, c, :], z[:, c, :], ACT.Relu, bias=bm_sb[:, c:c + 1])
                    ins.then_inc(relu_ok, 1)
                if live(s - 2):
                    b = s - 2
                    act.wait_ge(t_mm, CT * b + 2)
                    act.activation(xT[:, 1, :, :].rearrange("p k t -> p (k t)"), TP[:, :], ACT.Copy).then_inc(xT_ok, 1)
                    act.wait_ge(ra_ok, b + 1)
                    wait(act, s_ra2, 5 * b)
                    for j in range(CT):
                        ins = act.activation(ex[:, j, :], m8[:, j, :], ACT.Exp, bias=nm[:, j:j + 1],
                                             accum_out=Z[:, j:j + 1])
                    ins.then_inc(ex_ok, 1)

            act.wait_ge(ld_const, 16 * 8)
            act.wait_ge(st_empty, 32)
            act.wait_ge(c_pool, INIT_OPS)
            steps(act, step)

            def split_w(M, sl, par):
                act.wait_ge(ld_w[par], 8 * (M - par) + 16)
                wait(act, fc2_mm, M - 3)
                act.activation(w_hi[:, sl, :], w_raw[:, par, :], ACT.Copy).then_inc(w_hi_ok, 1)

            def gelu(M, e, m):
                for n in range(2):
                    wait(act, h_ready, 2 * M + (n - 1))
                    wait_apart(act, apart, fc1_mm, 2 * M + (n + 1))
                    act.activation(h_raw[:, n, :], HB[n][:, 0:NH], ACT.Gelu, bias=b1_sb[:, bass.ds(16 * e + m, 1)])\
                        .then_inc(gelu_ok, 1)

            for M in range(3):
                split_w(M, M % RING_W, M % 2)

            def expert(e, first, last):
                for half in range(2):
                    i = 2 * e + half
                    tail = last and half == 1
                    for u in range(4):
                        gelu(16 * i + u, e, u)
                        split_w(16 * i + (u + 3), (u + 3) % RING_W, (u + 3) % 2)
                    with act.Fori(1, 3) as g:
                        for u in range(4):
                            gelu(16 * i + 4 * g + u, e, 4 * g + u)
                            split_w(16 * i + 4 * g + (u + 3), (u + 3) % RING_W, (u + 3) % 2)
                    for u in range(4):
                        m = 12 + u
                        gelu(16 * i + m, e, m)
                        if not tail or m + 3 < MC:
                            split_w(16 * i + (m + 3), (u + 3) % RING_W, (u + 3) % 2)

            experts(act, expert)

        @block.tensor
        def _(pe):
            pe.wait_ge(ld_const, 16 * 8)
            pe.wait_ge(c_pool, INIT_OPS)
            pe.wait_ge(c_dve, CT)

            def transposes(b, j):
                wait(pe, xT_ok, CT * b + j)
                for k in range(KC):
                    ins = pe.transpose(TP[:, k * P:(k + 1) * P], xn2[:, j, k * P:(k + 1) * P], ident[:, :])
                ins.then_inc(t_mm, 1)

            def logits(b, j):
                pe.wait_ge(xT_ok, CT * b + (j + 1))
                for k in range(KC):
                    ins = pe.matmul(lg_ps[:, j, :], xT[:, j, k, :], rw_sb[:, k, :], start=(k == 0), stop=(k == KC - 1))
                return ins

            def step(s, r):
                q, q1 = r % 2, (r + 1) % 2
                if live(s):
                    pe.wait_ge(xn_ok, s + 1)
                    wait(pe, uv_ok, s)
                    for c in range(CT):
                        ins = pe.matmul(KB[:, :], wk_rep[:, c, :], xn[:, q, c, :], start=(c == 0), stop=(c == CT - 1))
                    ins.then_inc(kb_mm, 1)
                    wait(pe, s_ra, 3 * (s - 2) - 2)
                    for k in range(KC):
                        for c in range(CT):
                            ins = pe.matmul(q_ps[:, k:k + 1], xn[:, q, c, k * P:(k + 1) * P], wq_sb[:, c:c + 1],
                                            start=(c == 0), stop=(c == CT - 1))
                    ins.then_inc(q_mm, 1)
                    wait(pe, yT_ok, s)
                    for k in range(KC):
                        for c in range(CT):
                            ins = pe.matmul(Y[k // 2][:, (k % 2) * C:(k % 2 + 1) * C], xn[:, q, c, k * P:(k + 1) * P],
                                            adj_sb[:, c, :], start=(c == 0), stop=(c == CT - 1))
                    ins.then_inc(y_mm, 1)
                if live(s - 3):
                    b = s - 3
                    pe.wait_ge(oh_ok, b + 1)
                    wait(pe, s_rb, 6 * b)
                    if live(s):
                        pe.wait_ge(q_read, s + 1)
                    else:
                        pe.wait_ge(s_ra, 3 * (b + 1) - 2)
                    for j in range(CT):
                        to = rank_ps[:, j * 2 * E:(j + 1) * 2 * E]
                        pe.matmul(to, lower[:, :], onehot[:, j, :], start=True, stop=False)
                        for jj in range(j):
                            pe.matmul(to, ones[:, :], onehot[:, jj, :], start=False, stop=False)
                        ins = pe.matmul(to, ones[:, :], seen[:, :], start=False, stop=True)
                    ins.then_inc(rank_mm, 1)
                if live(s - 1):
                    b = s - 1
                    pe.wait_ge(yT_ok, b + 1)
                    wait(pe, z_ok, b)
                    for k in range(KC):
                        pe.wait_ge(att_ok, KC * b + (k + 1))
                        for c in range(CT):
                            ins = pe.matmul(AG[c][:, :], yT[:, q1, k, c * P:(c + 1) * P], att[:, k, :],
                                            start=(k == 0), stop=(k == KC - 1))
                    ins.then_inc(ag_mm, 1)
                if live(s - 2):
                    pe.wait_ge(xn2_ok, s - 1)
                    transposes(s - 2, 0)
                if live(s - 1):
                    pe.wait_ge(asum_ok, s)
                    wait(pe, rden_ok, s - 1)
                    pe.matmul(DEN[:, :], ones[:, :], asum[:, :], start=True, stop=True).then_inc(den_mm, 1)
                if live(s - 2):
                    b = s - 2
                    transposes(b, 1)
                    wait(pe, s_rb, 6 * (b - 1) + 1)
                    if live(s):
                        pe.wait_ge(q_read, s + 1)
                    logits(b, 0)
                    logits(b, 1).then_inc(lg_mm, 1)

            steps(pe, step)
            pe.wait_ge(s_rb, 6 * B)
            pe.matmul(cnt_ps, ones[:, :], seen[:, 0:E], start=True, stop=True).then_inc(cnt_mm, 1)

            def tok_transpose(i, e, half, t):
                pe.wait_ge(ga[half], 16 * TT * (e + 1))
                wait(pe, tok_ready, TT * i + t)
                for k in range(KC):
                    ins = pe.transpose(TB[:, k * TM:(k + 1) * TM], rows[0:TM, half, t, k * P:(k + 1) * P],
                                       ident[0:TM, 0:TM])
                ins.then_inc(tok_mm, 1)

            def fc1(i, M, half, sl):
                pe.wait_ge(w_ready, M + 1)
                for n in range(2):
                    wait(pe, gelu_ok, 2 * M + (n - 1))
                    cols = slice(n * NH, (n + 1) * NH)
                    for k in range(KC):
                        wk_ = slice(k * P, (k + 1) * P)
                        for a, t in ((w_hi, t_hi), (w_hi, t_lo), (w_lo, t_hi)):
                            ins = pe.matmul(HB[n][:, 0:NH], a[:, sl, wk_], t[:, half, k, cols],
                                            start=(k == 0 and a is w_hi and t is t_hi),
                                            stop=(k == KC - 1 and a is w_lo))
                    ins.then_inc(fc1_mm, 1)

            def fc2(M, sl, par, start, stop):
                pe.wait_ge(h_ready, 2 * M + 2)
                for t in range(TT):
                    cols = slice(t * TM, (t + 1) * TM)
                    for a, w in ((h_hi, w_hi), (h_hi, w_lo), (h_lo, w_hi)):
                        ins = pe.matmul(YB[t][0:TM, :], a[:, par, cols], w[:, sl, N:2 * N],
                                        start=(start and a is h_hi and w is w_hi), stop=(stop and a is h_lo))
                ins.then_inc(fc2_mm, 1)

            pe.wait_ge(cnt_ok, 1)
            for t in range(TT):
                tok_transpose(0, 0, 0, t)

            def expert(e, first, last):
                for half in range(2):
                    i = 2 * e + half
                    tail = last and half == 1
                    ne, nh = (e + 1, 0) if half else (e, 1)
                    for u in range(4):
                        if u == 0:
                            pe.wait_ge(tok_ready, TT * i + TT)
                        fc1(i, 16 * i + u, half, u)
                        if u == 0 and not (first and half == 0):
                            fc2(16 * i - 1, 3, 1, False, True)
                        if u > 0:
                            if u == 1:
                                wait(pe, y_read, TT * i)
                            fc2(16 * i + (u - 1), u - 1, (u - 1) % 2, u == 1, False)
                    with pe.Fori(1, 3) as g:
                        for u in range(4):
                            fc1(i, 16 * i + 4 * g + u, half, u)
                            fc2(16 * i + 4 * g + (u - 1), (u - 1) % 4, (u - 1) % 2, False, False)
                    for u in range(4):
                        m = 12 + u
                        todo = () if tail else TOK_AT.get(m, ())
                        for t in todo[0:1]:
                            tok_transpose(i + 1, ne, nh, t)
                        fc1(i, 16 * i + m, half, u)
                        for t in todo[1:2]:
                            tok_transpose(i + 1, ne, nh, t)
                        fc2(16 * i + (m - 1), (u - 1) % 4, (u - 1) % 2, False, False)

            experts(pe, expert)
            fc2(16 * PASSES - 1, 3, 1, False, True)


TOK_AT = {12: (0, 1), 13: (2, 3), 14: (4,)}


def kernel(**inputs):
    import numpy as np
    import concourse.bacc as bacc
    from concourse.bass_utils import run_bass_kernel_spmd

    g = {k: np.asarray(v) for k, v in inputs.items()}
    fc1 = g["L0_ffn_fc1_w"].reshape(E, MC, P, KC, P).transpose(0, 1, 4, 3, 2).reshape(E, MC, P, N)
    fc2 = g["L0_ffn_fc2_w"].reshape(E, N, MC, P).transpose(0, 2, 3, 1)
    arrays = {
        "x": g["x"],
        "adj_t": g["adj"].T,
        "wq": g["L0_gnn_wq"],
        "wk": g["L0_gnn_wk"],
        "bm": g["L0_gnn_bm"],
        "router_wt": g["L0_ffn_router_w"].T,
        "router_b": g["L0_ffn_router_b"],
        "w_cat": np.concatenate([fc1, fc2], axis=3),
        "fc1_b": g["L0_ffn_fc1_b"].reshape(E * MC, P).T,
        "fc2_b": g["L0_ffn_fc2_b"],
        "scale": g["L0_ffn_layer_scale"],
    }
    nc = bacc.Bacc("TRN2", target_bir_lowering=False, num_devices=1)
    arrays = {k: np.ascontiguousarray(v) for k, v in arrays.items()}
    args = [nc.dram_tensor(k, v.shape, F32, kind="ExternalInput").ap() for k, v in arrays.items()]
    out = nc.dram_tensor("out", (B, C, N), F32, kind="ExternalOutput").ap()
    gnn_moe_kernel(nc, *args, out)
    r = run_bass_kernel_spmd(nc, [arrays], core_ids=[0])
    return r.results[0]["out"]
```

```python
from contextlib import ExitStack

import concourse.bass as bass
from concourse import mybir

ALU = mybir.AluOpType
ACT = mybir.ActivationFunctionType
AX = mybir.AxisListType
F32 = mybir.dt.float32
F32R = mybir.dt.float32r
I32 = mybir.dt.int32
U32 = mybir.dt.uint32

P = 128
B, C, N = 32, 256, 512
CT = C // P
KC = N // P
E, H = 8, 2048
TOKENS = B * C
CAP = int(1.2 * (TOKENS // E + 1))
TT = 5
TM = CAP // (2 * TT)
HALF = TT * TM
HP = HALF + HALF % 2
NH = HP // 2
MC = H // P
S1 = 9472
S2 = TOKENS
TAB2 = E * S1
ROWS = TAB2 + E * S2
BIG = 1 << 22
EPS_LN = 1e-5
EPS_W = 1e-9
SLOPE = 0.01
RING_X = 4
RING_W = 4
PASSES = 2 * E
INIT_OPS = 18
assert S1 >= TOKENS + CAP and HALF * 2 == CAP


def wait(eng, sem, value):
    if isinstance(value, int) and value <= 0:
        return
    eng.wait_ge(sem, value)


def wait_apart(eng, apart, sem, value):
    wait(eng, sem, value)
    eng.sem_inc(apart, 1)


class Chain:

    def __init__(self, eng, sem, per, rnd):
        self.eng, self.sem, self.per, self.base, self.n = eng, sem, per, per * rnd, 0

    def __call__(self, ins, apart=None):
        ins.then_inc(self.sem, 1)
        self.n += 1
        if apart is None:
            self.eng.wait_ge(self.sem, self.base + self.n)
        else:
            wait_apart(self.eng, apart, self.sem, self.base + self.n)

    def end(self):
        assert self.n == self.per, (self.n, self.per)


def gnn_moe_kernel(nc, x, adj_t, wq, wk, bm, router_wt, router_b, w_cat, fc1_b, fc2_b, scale, out):
    xn_dram = nc.dram_tensor("xn_rows", (TOKENS, N), F32).ap()
    table = nc.dram_tensor("slot_table", (ROWS, 2), I32).ap()

    with ExitStack() as ctx:
        def sb(name, shape, dt=F32):
            return ctx.enter_context(nc.sbuf_tensor(name, shape, dt))

        def psum(name, shape):
            return ctx.enter_context(nc.psum_tensor(name, shape, F32))

        def sem(name):
            return ctx.enter_context(nc.semaphore(name))

        ident = sb("ident", [P, P])
        lower = sb("lower", [P, P])
        ones = sb("ones", [P, P])
        iota8 = sb("iota8", [P, E])
        stride_k = sb("stride_k", [P, 2 * CT])
        base_k = sb("base_k", [P, 2 * CT])
        tok_f = sb("tok_f", [P, CT])
        adj_sb = sb("adj_sb", [P, CT, C])
        wq_sb = sb("wq_sb", [P, CT])
        wk_sb = sb("wk_sb", [P, CT])
        wk_rep = sb("wk_rep", [P, CT, P])
        bm_sb = sb("bm_sb", [P, CT])
        rw_sb = sb("rw_sb", [P, KC, E])
        rb_sb = sb("rb_sb", [P, CT, E])
        b1_sb = sb("b1_sb", [P, E * MC])

        X = sb("X", [P, RING_X, CT, N])
        xn = sb("xn", [P, 2, CT, N])
        yT = sb("yT", [P, 2, KC, C])
        uv = sb("uv", [P, 2, N])
        fB = sb("fB", [P, 2, N])
        fD = sb("fD", [P, 2, N])
        asum = sb("asum", [P, N])
        rden = sb("rden", [P, N])
        x2 = sb("x2", [P, 2, CT, N])
        st1 = sb("st1", [P, CT, 6])
        mv1 = sb("mv1", [P, 2, CT, 2])
        ve1 = sb("ve1", [P, CT])
        rs1 = sb("rs1", [P, 2, CT])
        st2 = sb("st2", [P, CT, 6])
        mv2 = sb("mv2", [P, CT, 2])
        ve2 = sb("ve2", [P, CT])
        rs2 = sb("rs2", [P, CT])
        mhalf = sb("mhalf", [P, CT])
        qs = sb("qs", [P, 2, KC])
        qr = sb("qr", [P, 1])
        qm = sb("qm", [P, 1])
        nq = sb("nq", [P, 2])
        fA = sb("fA", [P, 2, KC])
        fC = sb("fC", [P, 2, KC])
        lg = sb("lg", [P, CT, E])
        m8 = sb("m8", [P, CT, 8])
        i8 = sb("i8", [P, CT, 8], U32)
        nm = sb("nm", [P, CT])
        ex = sb("ex", [P, CT, 8])
        Z = sb("Z", [P, CT])
        zz = sb("zz", [P, CT])
        zr = sb("zr", [P, CT])
        i2 = sb("i2", [P, CT, 2])
        w2 = sb("w2", [P, CT, 2])
        ok = sb("ok", [P, CT, 2])
        onehot = sb("onehot", [P, CT, 2 * E])
        seen = sb("seen", [P, 2, CT, 2 * E])
        prod = sb("prod", [P, 2 * CT, E])
        pos = sb("pos", [P, 2 * CT])
        dst = sb("dst", [P, 2 * CT])
        dst_i = sb("dst_i", [P, 2, 2 * CT], U32)
        pay = sb("pay", [P, 2, 2 * CT, 2], I32)
        cnt = sb("cnt", [P, E], I32)

        w_raw = sb("w_raw", [P, 2, 2 * N])
        w_hi = sb("w_hi", [P, RING_W, 2 * N], F32R)
        w_lo = sb("w_lo", [P, RING_W, 2 * N], F32R)
        t_hi = sb("t_hi", [P, 2, KC, HP], F32R)
        t_lo = sb("t_lo", [P, 2, KC, HP], F32R)
        h_raw = sb("h_raw", [P, 2, NH])
        h_hi = sb("h_hi", [P, 2, HP], F32R)
        h_lo = sb("h_lo", [P, 2, HP], F32R)
        rows = sb("rows", [P, 2, TT, N])
        yo = sb("yo", [P, TT, N])
        b2_sb = sb("b2_sb", [P, 2, N])
        ls_sb = sb("ls_sb", [P, 2, N])
        slots = sb("slots", [P, 2, TT, 2], I32)

        flat = rows[:, :, :, :].rearrange("p a t n -> p (a t n)")
        tq = flat[:, 0:KC * N].rearrange("p (k n) -> p k n", k=KC)
        att = flat[:, KC * N:2 * KC * N].rearrange("p (k n) -> p k n", k=KC)
        yflat = yo[:, :, :].rearrange("p t n -> p (t n)")
        z = yflat[:, 0:CT * N].rearrange("p (c n) -> p c n", c=CT)
        xT = yflat[:, CT * N:2 * CT * N].rearrange("p (j k t) -> p j k t", j=CT, k=KC)
        xn2 = sb("xn2", [P, CT, N])
        empty = flat[0:E, 0:2 * CAP].bitcast(I32)

        bank = [psum(f"bank{i}", [P, N]) for i in range(8)]
        KB = bank[0]
        Y = [bank[1], bank[2]]
        AG = [bank[3], bank[4]]
        DEN = bank[0]
        TP = [bank[5], bank[6]]
        SM = bank[7]
        q_ps = SM[:, 0:KC]
        lg_ps = SM[:, 16:16 + CT * E].rearrange("p (j e) -> p j e", j=CT)
        rank_ps = SM[:, 32:32 + CT * 2 * E]
        cnt_ps = SM[:, 64:64 + E]
        YB = bank[0:TT]
        HB = bank[TT:TT + 2]
        TB = bank[7]

        ld_const = sem("ld_const")
        ld_x = [sem(f"ld_x{i}") for i in range(RING_X)]
        st_x2 = [sem(f"st_x2{i}") for i in range(2)]
        st_xn = sem("st_xn")
        st_empty = sem("st_empty")
        sc_tab = [sem(f"sc_tab{i}") for i in range(2)]
        cp_first = sem("cp_first")
        cp_tab = sem("cp_tab")
        ld_w = [sem(f"ld_w{i}") for i in range(2)]
        ld_slots = [sem(f"ld_slots{i}") for i in range(2)]
        ld_b2 = [sem(f"ld_b2{i}") for i in range(2)]
        ga = [sem(f"ga{i}") for i in range(2)]
        sc_out = sem("sc_out")
        c_pool = sem("c_pool")
        apart = sem("apart")
        empty_ok = sem("empty_ok")
        pow1 = sem("pow1")
        pow2 = sem("pow2")
        qmax = sem("qmax")
        asum_ok = sem("asum_ok")
        pool_sum = sem("pool_sum")
        x2_ok = sem("x2_ok")
        ls_ok = sem("ls_ok")
        y_res = sem("y_res")
        c_dve = sem("c_dve")
        var1 = sem("var1")
        s_st1 = sem("s_st1")
        xn_ok = sem("xn_ok")
        q_read = sem("q_read")
        q_red = sem("q_red")
        uv_ok = sem("uv_ok")
        att_ok = sem("att_ok")
        rden_ok = sem("rden_ok")
        z_ok = sem("z_ok")
        s_st2 = sem("s_st2")
        var2 = sem("var2")
        xn2_ok = sem("xn2_ok")
        s_ra = sem("s_ra")
        s_ra2 = sem("s_ra2")
        oh_ok = sem("oh_ok")
        ra_ok = sem("ra_ok")
        lg_read = sem("lg_read")
        rank_read = sem("rank_read")
        pos_ok = sem("pos_ok")
        nq_ok = sem("nq_ok")
        route_ok = sem("route_ok")
        cnt_ok = sem("cnt_ok")
        w_ready = sem("w_ready")
        tok_hi = sem("tok_hi")
        tok_ready = sem("tok_ready")
        h_hi_ok = sem("h_hi_ok")
        h_ready = sem("h_ready")
        y_read = sem("y_read")
        y_scaled = sem("y_scaled")
        tq_ok = sem("tq_ok")
        yT_ok = sem("yT_ok")
        fac_ok = sem("fac_ok")
        relu_ok = sem("relu_ok")
        xT_ok = sem("xT_ok")
        ex_ok = sem("ex_ok")
        w_hi_ok = sem("w_hi_ok")
        gelu_ok = sem("gelu_ok")
        kb_mm = sem("kb_mm")
        q_mm = sem("q_mm")
        y_mm = sem("y_mm")
        rank_mm = sem("rank_mm")
        ag_mm = sem("ag_mm")
        den_mm = sem("den_mm")
        t_mm = sem("t_mm")
        lg_mm = sem("lg_mm")
        cnt_mm = sem("cnt_mm")
        tok_mm = sem("tok_mm")
        fc1_mm = sem("fc1_mm")
        fc2_mm = sem("fc2_mm")

        FIRST, LAST = 6, 30
        STEPS = B + 4

        def steps(eng, step):
            for s in range(-1, FIRST):
                step(s, s % 4)
            with eng.Fori(0, (LAST - FIRST) // 4) as j:
                for u in range(4):
                    step(4 * j + (FIRST + u), (FIRST + u) % 4)
            for s in range(LAST, STEPS):
                step(s, s % 4)

        def live(b):
            return not isinstance(b, int) or 0 <= b < B

        def experts(eng, expert):
            expert(0, True, False)
            with eng.Fori(1, E - 1) as e:
                expert(e, False, False)
            expert(E - 1, False, True)

        block = ctx.enter_context(nc.Block())

        @block.sync
        def _(sp):
            consts = [
                (adj_sb[:, :, :], adj_t.rearrange("(k p) o -> p k o", p=P)),
                (wq_sb[:, :], wq.rearrange("(k p) -> p k", p=P)),
                (wk_sb[:, :], wk.rearrange("(k p) -> p k", p=P)),
                (bm_sb[:, :], bm.rearrange("(k p) -> p k", p=P)),
                (rw_sb[:, :, :], router_wt.rearrange("(k p) e -> p k e", p=P)),
                (rb_sb[:, 0, :], router_b.rearrange("(a e) -> a e", a=1).to_broadcast([P, E])),
                (rb_sb[:, 1, :], router_b.rearrange("(a e) -> a e", a=1).to_broadcast([P, E])),
                (b1_sb[:, :], fc1_b),
            ]

            def load_x(b, r):
                wait_apart(sp, apart, x2_ok, CT * (b - (RING_X - 1)))
                sp.dma_start(X[:, r, :, :], x[b].rearrange("(c p) n -> p c n", p=P)).then_inc(ld_x[r], 16)

            load_x(0, 0)
            with nc.allow_non_contiguous_dma(reason="small constants"):
                for dst_ap, src_ap in consts:
                    sp.dma_start(dst_ap, src_ap).then_inc(ld_const, 16)
            load_x(1, 1)
            sp.wait_ge(empty_ok, 1)
            for part, stride in ((0, S1), (TAB2, S2)):
                to = table[part:part + E * stride, :].rearrange("(e s) w -> e (s w)", e=E)[:, 0:2 * CAP]
                sp.dma_start(to, empty).then_inc(st_empty, 16)
            for k in range(2):
                sp.dma_start(w_raw[:, k, :], w_cat[0, k]).then_inc(ld_w[k], 16)

            out_b = out.rearrange("b (c p) n -> b p c n", p=P)
            xn_b = xn_dram.rearrange("(b c p) n -> b p c n", c=CT, p=P)

            def step(s, r):
                if live(s + 2) and not (isinstance(s, int) and s < 0):
                    load_x(s + 2, (r + 2) % 4)
                if live(s - 2):
                    wait_apart(sp, apart, xn2_ok, s - 1)
                    sp.dma_start(xn_b[s - 2], xn2[:, :, :]).then_inc(st_xn, 16)
                if live(s - 1):
                    wait_apart(sp, apart, x2_ok, CT * s)
                    sp.dma_start(out_b[s - 1], x2[:, (r + 1) % 2, :, :]).then_inc(st_x2[(r + 1) % 2], 16)

            steps(sp, step)

            for i in range(2):
                sp.wait_ge(sc_tab[i], 16 * 2 * CT * B // 2)
            sp.wait_ge(cnt_ok, 1)
            def copy_second(e, done):
                with sp.register(f"first_choices{e}") as reg:
                    sp.reg_load(reg, cnt[0:1, e:e + 1])
                    n1 = sp.snap(reg, min_val=0, max_val=TOKENS)
                    sp.dma_start(table[bass.ds(n1 + e * S1, CAP), :],
                                 table[TAB2 + e * S2:TAB2 + e * S2 + CAP, :]).then_inc(done, 16)

            copy_second(0, cp_first)
            sp.wait_ge(st_xn, 16 * B)
            sp.wait_ge(cp_first, 16)

            def load_pass(e, half):
                i = 2 * e + half
                wait_apart(sp, apart, y_scaled, TT * (i - 1))
                wait_apart(sp, apart, sc_out, 16 * TT * (i - 1))
                base = e * S1 + half * HALF
                sp.dma_start(slots[0:TM, half, :, :],
                             table[bass.ds(base, HALF), :].rearrange("(p t) w -> p t w", t=TT))\
                    .then_inc(ld_slots[half], 16)
                for dst_ap, src_ap in ((b2_sb, fc2_b), (ls_sb, scale)):
                    sp.dma_start(dst_ap[:, half, :], src_ap[bass.ds(e, 1), :].to_broadcast([P, N]))\
                        .then_inc(ld_b2[half], 16)

            def load_w(i_next, e, m, par):
                wait_apart(sp, apart, w_ready, i_next - 1)
                sp.dma_start(w_raw[:, par, :], w_cat[e, m]).then_inc(ld_w[par], 16)

            load_pass(0, 0)
            load_pass(0, 1)

            def expert(e, first, last):
                for half in range(2):
                    i = 2 * e + half
                    with sp.Fori(1, 5) as g:
                        for u in range(2):
                            load_w(16 * i + 2 * g + u, e, 2 * g + u, u)
                    if first and half == 0:
                        for ee in range(1, E):
                            copy_second(ee, cp_tab)
                    elif first:
                        sp.wait_ge(cp_tab, 16 * (E - 1))
                    if not (first and half == 0 or last and half == 1):
                        load_pass(e + half, 1 - half)
                    with sp.Fori(5, MC // 2) as g:
                        for u in range(2):
                            load_w(16 * i + 2 * g + u, e, 2 * g + u, u)
                    if half == 0 or not last:
                        for u in range(2):
                            load_w(16 * i + (MC + u), e + half, u, u)

            experts(sp, expert)
            sp.wait_ge(sc_out, 16 * TT * PASSES)

        @block.gpsimd
        def _(pool):
            pc = Chain(pool, c_pool, INIT_OPS, 0)
            pc(pool.memset(flat[:, 2 * KC * N:], 0.0))
            pc(pool.memset(flat[0:E, 0:2 * CAP], 0.0))
            pc(pool.memset(flat[0:E, 0:2 * CAP].bitcast(I32).rearrange("p (s w) -> p s w", w=2)[:, :, 0:1], BIG))
            pool.memset(ones[:, :], 1.0).then_inc(empty_ok, 1)
            pc(pool.memset(ident[:, :], 0.0))
            pc(pool.affine_select(out=ident[:, :], in_=ident[:, :], compare_op=ALU.not_equal, fill=1.0,
                                  base=0, pattern=[[-1, P]], channel_multiplier=1))
            pc(pool.memset(lower[:, :], 1.0))
            pc(pool.affine_select(out=lower[:, :], in_=lower[:, :], compare_op=ALU.is_gt, fill=0.0,
                                  base=0, pattern=[[1, P]], channel_multiplier=-1))
            pc(pool.iota(iota8[:, :], pattern=[[1, E]], base=0, channel_multiplier=0,
                         allow_small_or_imprecise_dtypes=True))
            pc(pool.iota(tok_f[:, :], pattern=[[P, CT]], base=0, channel_multiplier=1,
                         allow_small_or_imprecise_dtypes=True))
            pc(pool.memset(mhalf[:, :], -0.5))
            pc(pool.memset(seen[:, :, :, :], 0.0))
            for k, (stride, base) in enumerate(((S1, 0), (S2, TAB2))):
                pc(pool.memset(stride_k[:, k::2], float(stride)))
                pc(pool.memset(base_k[:, k::2], float(base + BIG)))
            pc(pool.memset(t_hi[:, :, :, HALF:HP].bitcast(F32), 0.0))
            pc(pool.memset(t_lo[:, :, :, HALF:HP].bitcast(F32), 0.0))
            pc(pool.memset(h_raw[:, :, :], 0.0))
            pc.end()

            def step(s, r):
                if live(s - 1):
                    b = s - 1
                    pch = Chain(pool, pool_sum, 2, b)
                    wait(pool, den_mm, b)
                    wait(pool, att_ok, KC * b + 2)
                    pch(pool.tensor_tensor(asum[:, :], att[:, 0, :], att[:, 1, :], ALU.add))
                    wait(pool, att_ok, KC * b + 3)
                    pch(pool.tensor_tensor(asum[:, :], asum[:, :], att[:, 2, :], ALU.add))
                    pch.end()
                    wait(pool, att_ok, KC * b + 4)
                    pool.tensor_tensor(asum[:, :], asum[:, :], att[:, 3, :], ALU.add).then_inc(asum_ok, 1)
                if live(s):
                    wait(pool, fac_ok, s)
                    wait_apart(pool, apart, q_red, s + 1)
                    pool.partition_all_reduce(qm[:, :], qr[:, :], P, bass.bass_isa.ReduceOp.max).then_inc(qmax, 1)
                if live(s - 2):
                    wait(pool, var2, s - 1)
                    wait(pool, xn2_ok, s - 2)
                    pool.tensor_tensor(rs2[:, :], ve2[:, :], mhalf[:, :], ALU.pow).then_inc(pow2, 1)
                if live(s - 4):
                    q = r % 2
                    wait_apart(pool, apart, route_ok, s - 3)
                    if isinstance(s, int) and s == 4:
                        pool.wait_ge(st_empty, 32)
                    for k in range(2 * CT):
                        pool.indirect_dma_start(
                            out=table[:, :], out_offset=bass.IndirectOffsetOnAxis(ap=dst_i[:, q, k:k + 1], axis=0),
                            in_=pay[:, q, k, :], in_offset=None, bounds_check=ROWS - 1, oob_is_err=False,
                        ).then_inc(sc_tab[q], 16)
                if live(s + 1):
                    wait(pool, var1, s + 2)
                    pool.tensor_tensor(rs1[:, (r + 1) % 2, :], ve1[:, :], mhalf[:, :], ALU.pow).then_inc(pow1, 1)
                if live(s - 1):
                    b, q = s - 1, (r + 1) % 2
                    wait(pool, st_x2[q], 8 * (b - q))
                    wait(pool, xn2_ok, b - 1)
                    for c in range(CT):
                        wait(pool, relu_ok, CT * b + (c + 1))
                        pool.tensor_tensor(x2[:, q, c, :], z[:, c, :], X[:, (r + 3) % 4, c, :], ALU.add)\
                            .then_inc(x2_ok, 1)

            steps(pool, step)

            def gather(e, half):
                i = 2 * e + half
                wait_apart(pool, apart, ld_slots[half], 16 * (e + 1))
                for t in range(TT):
                    pool.indirect_dma_start(
                        out=rows[0:TM, half, t, :], out_offset=None, in_=xn_dram[:, :],
                        in_offset=bass.IndirectOffsetOnAxis(ap=slots[0:TM, half, t, 0:1].bitcast(U32), axis=0),
                        bounds_check=TOKENS - 1, oob_is_err=False,
                    ).then_inc(ga[half], 16)

            gather(0, 0)
            gather(0, 1)

            for i in range(2):
                pool.wait_ge(st_x2[i], 16 * B // 2)

            def finish(e, half):
                i = 2 * e + half
                for t in range(TT):
                    pool.wait_ge(ls_ok, TT * i + (t + 1))
                    pool.tensor_tensor(yo[0:TM, t, :], yo[0:TM, t, :], rows[0:TM, half, t, :], ALU.add)\
                        .then_inc(y_res, 1)
                for t in range(TT):
                    wait_apart(pool, apart, y_scaled, TT * i + (t + 1))
                    if t == 0:
                        wait_apart(pool, apart, sc_out, 16 * TT * i)
                    pool.indirect_dma_start(
                        out=out.rearrange("b c n -> (b c) n"),
                        out_offset=bass.IndirectOffsetOnAxis(ap=slots[0:TM, half, t, 0:1].bitcast(U32), axis=0),
                        in_=yo[0:TM, t, :], in_offset=None, bounds_check=TOKENS - 1, oob_is_err=False,
                        compute_op=ALU.add,
                    ).then_inc(sc_out, 16)

            def expert(e, first, last):
                for half in range(2):
                    finish(e, half)
                    if not last:
                        gather(e + 1, half)

            experts(pool, expert)

        @block.vector
        def _(dve):
            dve.wait_ge(c_pool, INIT_OPS)
            dve.wait_ge(ld_const, 16 * 8)
            for k in range(CT):
                dve.tensor_scalar(wk_rep[:, k, :], ones[:, :], wk_sb[:, k:k + 1], None, ALU.mult).then_inc(c_dve, 1)

            def step(s, r):
                q, q1 = r % 2, (r + 1) % 2
                if live(s - 3):
                    wait(dve, lg_mm, s - 2)
                    dve.tensor_tensor(lg[:, :, :], lg_ps, rb_sb[:, :, :], ALU.add).then_inc(lg_read, 1)
                if live(s - 4):
                    wait(dve, rank_mm, s - 3)
                    oh = onehot[:, :, :].rearrange("p j (k e) -> p (j k) e", k=2)
                    dve.tensor_tensor(prod[:, :, :], rank_ps.rearrange("p (a e) -> p a e", e=E), oh, ALU.mult)\
                        .then_inc(rank_read, 1)
                if live(s - 1):
                    b = s - 1
                    wait(dve, fac_ok, b + 1)
                    wait(dve, ag_mm, b)
                    wait(dve, asum_ok, b)
                    for k in range(KC):
                        wait(dve, tq_ok, KC * b + k + 1)
                        dve.scalar_tensor_tensor(out=att[:, k, :], in0=fD[:, q1, :], scalar=fC[:, q1, k:k + 1],
                                                 in1=tq[:, k, :], op0=ALU.mult, op1=ALU.max).then_inc(att_ok, 1)
                if live(s - 4):
                    b = s - 4
                    wait(dve, rank_read, b + 1)
                    dve.tensor_reduce(pos[:, :], prod[:, :, :], AX.X, ALU.add).then_inc(pos_ok, 1)
                    wait(dve, pos_ok, b + 1)
                    dve.tensor_tensor(dst_i[:, q, :], dst[:, :], pos[:, :], ALU.add).then_inc(route_ok, 1)
                if live(s):
                    wait(dve, q_mm, s + 1)
                    wait(dve, fac_ok, s - 1)
                    dve.tensor_copy(qs[:, q, :], q_ps).then_inc(q_read, 1)
                    dve.wait_ge(q_read, s + 1)
                    wait(dve, qmax, s)
                    dve.reduce_max(qr[:, :], qs[:, q, :], AX.X).then_inc(q_red, 1)
                if live(s - 2):
                    b = s - 2
                    wait(dve, x2_ok, CT * (b + 1))
                    wait(dve, pow2, b)
                    ch = Chain(dve, s_st2, 2, b)
                    for c in range(CT):
                        ins = dve.bn_stats(st2[:, c, :], x2[:, q, c, :])
                    ch(ins, apart)
                    for c in range(CT):
                        ins = dve.bn_aggr(mv2[:, c, :], st2[:, c, :])
                    ch(ins)
                    ch.end()
                    dve.tensor_scalar(ve2[:, :], mv2[:, :, 1], EPS_LN, None, ALU.add).then_inc(var2, 1)
                if live(s - 3):
                    b = s - 3
                    wait(dve, ex_ok, b)
                    wait_apart(dve, apart, lg_read, b + 1)
                    ch = Chain(dve, s_ra, 2, b)
                    for j in range(CT):
                        ins = dve.max(m8[:, j, :], lg[:, j, :])
                    ch(ins, apart)
                    for j in range(CT):
                        ins = dve.max_index(i8[:, j, :], m8[:, j, :], lg[:, j, :])
                    ch(ins)
                    ch.end()
                    dve.tensor_copy(i2[:, :, :], i8[:, :, 0:2])
                    dve.tensor_scalar(nm[:, :], m8[:, :, 0], -1.0, None, ALU.mult).then_inc(ra_ok, 1)
                if live(s):
                    wait(dve, qmax, s + 1)
                    wait(dve, fac_ok, s)
                    dve.tensor_scalar(nq[:, 0:1], qm[:, :], -1.0, None, ALU.mult)
                    dve.tensor_scalar(nq[:, 1:2], qm[:, :], -SLOPE, None, ALU.mult).then_inc(nq_ok, 1)
                if live(s - 2):
                    b = s - 2
                    wait(dve, pow2, b + 1)
                    wait(dve, st_xn, 16 * b)
                    wait(dve, t_mm, CT * b)
                    for c in range(CT):
                        ins = dve.tensor_scalar(xn2[:, c, :], x2[:, q, c, :], mv2[:, c, 0:1], rs2[:, c:c + 1],
                                                ALU.subtract, ALU.mult)
                    ins.then_inc(xn2_ok, 1)
                if live(s + 1):
                    b, rb = s + 1, (r + 1) % 4
                    dve.wait_ge(ld_x[rb], 4 * b + (16 - 4 * rb))
                    wait(dve, pow1, b)
                    ch = Chain(dve, s_st1, 2, b)
                    for c in range(CT):
                        ins = dve.bn_stats(st1[:, c, :], X[:, rb, c, :])
                    ch(ins, apart)
                    for c in range(CT):
                        ins = dve.bn_aggr(mv1[:, q1, c, :], st1[:, c, :])
                    ch(ins)
                    ch.end()
                    dve.tensor_scalar(ve1[:, :], mv1[:, q1, :, 1], EPS_LN, None, ALU.add).then_inc(var1, 1)
                if live(s - 3):
                    b = s - 3
                    wait(dve, ex_ok, b + 1)
                    wait(dve, sc_tab[q1], 8 * 2 * CT * (b - q1))
                    ch = Chain(dve, s_ra2, 7, b)
                    i2f = i2[:, :, :].rearrange("p j k -> p (j k)")
                    dve.scalar_tensor_tensor(out=zz[:, :], in0=Z[:, :], scalar=EPS_W, in1=ex[:, :, 1],
                                             op0=ALU.mult, op1=ALU.add)
                    ch(dve.tensor_tensor(dst[:, :], i2f, stride_k[:, :], ALU.mult))
                    dve.tensor_scalar(zz[:, :], zz[:, :], 1.0, None, ALU.add)
                    ch(dve.tensor_tensor(dst[:, :], dst[:, :], base_k[:, :], ALU.add))
                    ch(dve.reciprocal(zr[:, :], zz[:, :]))
                    for k in range(2):
                        ins = dve.tensor_tensor(w2[:, :, k], ex[:, :, k], zr[:, :], ALU.mult)
                    ch(ins)
                    ch(dve.tensor_scalar(ok[:, :, :], w2[:, :, :], EPS_W, None, ALU.is_gt))
                    dve.scalar_tensor_tensor(out=dst[:, :], in0=ok[:, :, :].rearrange("p j k -> p (j k)"),
                                             scalar=-float(BIG), in1=dst[:, :], op0=ALU.mult, op1=ALU.add)
                    for j in range(CT):
                        for k in range(2):
                            ins = dve.tensor_scalar(onehot[:, j, k * E:(k + 1) * E], iota8[:, :], i2[:, j, k:k + 1],
                                                    ok[:, j, k:k + 1], ALU.is_equal, ALU.mult)
                    ch(ins)
                    dve.tensor_tensor(seen[:, q1, 1, :], seen[:, q1, 0, :], onehot[:, 0, :], ALU.add)
                    pj = pay[:, q1, :, :].rearrange("p (j k) w -> p j k w", k=2)
                    for k in range(2):
                        dve.tensor_copy(pj[:, :, k, 0], tok_f[:, :])
                    ch(dve.tensor_copy(pj[:, :, :, 1].bitcast(F32), w2[:, :, :]))
                    ch.end()
                    dve.tensor_scalar(tok_f[:, :], tok_f[:, :], float(C), None, ALU.add)
                    wait(dve, rank_mm, b)
                    dve.tensor_tensor(seen[:, q, 0, :], seen[:, q1, 1, :], onehot[:, 1, :], ALU.add).then_inc(oh_ok, 1)
                if live(s + 1):
                    b, rb = s + 1, (r + 1) % 4
                    wait(dve, pow1, b + 1)
                    wait(dve, y_mm, b - 1)
                    for c in range(CT):
                        ins = dve.tensor_scalar(xn[:, q1, c, :], X[:, rb, c, :], mv1[:, q1, c, 0:1],
                                                rs1[:, q1, c:c + 1], ALU.subtract, ALU.mult)
                    ins.then_inc(xn_ok, 1)
                if live(s - 1):
                    wait(dve, den_mm, s)
                    wait(dve, z_ok, CT * (s - 1))
                    dve.reciprocal(rden[:, :], DEN[:, :]).then_inc(rden_ok, 1)
                if live(s - 1):
                    b = s - 1
                    wait(dve, rden_ok, b + 1)
                    wait(dve, x2_ok, CT * b)
                    wait(dve, ag_mm, b + 1)
                    for c in range(CT):
                        dve.tensor_tensor(z[:, c, :], AG[c][:, :], rden[:, :], ALU.mult).then_inc(z_ok, 1)

            steps(dve, step)

            dve.wait_ge(cnt_mm, 1)
            dve.tensor_copy(cnt[:, :], cnt_ps).then_inc(cnt_ok, 1)

            def split_w(M, sl, par):
                dve.wait_ge(w_hi_ok, M + 1)
                dve.tensor_tensor(w_lo[:, sl, :], w_raw[:, par, :], w_hi[:, sl, :].bitcast(F32), ALU.subtract)\
                    .then_inc(w_ready, 1)

            def split_tok(i, half, t, bank_=TB):
                dve.wait_ge(tok_mm, TT * i + (t + 1))
                src = bank_[:, 0:KC * TM].rearrange("p (k t) -> p k t", k=KC)
                hi = t_hi[:, half, :, t * TM:(t + 1) * TM]
                dve.tensor_copy(hi, src).then_inc(tok_hi, 1)
                dve.wait_ge(tok_hi, TT * i + (t + 1))
                dve.tensor_tensor(t_lo[:, half, :, t * TM:(t + 1) * TM], src, hi.bitcast(F32), ALU.subtract)\
                    .then_inc(tok_ready, 1)

            def split_h(M, par):
                wait(dve, fc2_mm, M - 1)
                for n in range(2):
                    dve.wait_ge(gelu_ok, 2 * M + (n + 1))
                    hi = h_hi[:, par, n * NH:(n + 1) * NH]
                    dve.tensor_copy(hi, h_raw[:, n, :]).then_inc(h_hi_ok, 1)
                    dve.wait_ge(h_hi_ok, 2 * M + (n + 1))
                    dve.tensor_tensor(h_lo[:, par, n * NH:(n + 1) * NH], h_raw[:, n, :], hi.bitcast(F32),
                                      ALU.subtract).then_inc(h_ready, 1)

            def read_y(e, half):
                i = 2 * e + half
                dve.wait_ge(fc2_mm, 16 * i + 16)
                dve.wait_ge(ld_b2[half], 32 * (e + 1))
                wait(dve, sc_out, 16 * TT * i)
                for t in range(TT):
                    dve.tensor_tensor(yo[0:TM, t, :], YB[t][0:TM, :], b2_sb[0:TM, half, :], ALU.add)\
                        .then_inc(y_read, 1)

            def scale_y(e, half):
                i = 2 * e + half
                for t in range(TT):
                    dve.wait_ge(y_read, TT * i + (t + 1))
                    dve.tensor_tensor(yo[0:TM, t, :], yo[0:TM, t, :], ls_sb[0:TM, half, :], ALU.mult)\
                        .then_inc(ls_ok, 1)

            def weigh_y(e, half):
                i = 2 * e + half
                for t in range(TT):
                    dve.wait_ge(y_res, TT * i + (t + 1))
                    dve.tensor_scalar(yo[0:TM, t, :], yo[0:TM, t, :], slots[0:TM, half, t, 1:2].bitcast(F32), None,
                                      ALU.mult).then_inc(y_scaled, 1)

            for M in range(2):
                split_w(M, M % RING_W, M % 2)
            for t in range(TT):
                split_tok(0, 0, t, YB[t])
            split_w(2, 2, 0)

            def expert(e, first, last):
                for half in range(2):
                    i = 2 * e + half
                    tail = last and half == 1
                    with_prev = not (first and half == 0)
                    pe_, ph = (e, 0) if half else (e - 1, 1)

                    def round_(m, u, w=True):
                        split_h(16 * i + m, u % 2)
                        if w:
                            split_w(16 * i + m + 3, (u + 3) % RING_W, (u + 3) % 2)

                    for u in range(4):
                        round_(u, u, w=u > 0)
                        if u == 0:
                            if with_prev:
                                read_y(pe_, ph)
                            split_w(16 * i + 3, 3, 1)
                        if u == 1 and with_prev:
                            scale_y(pe_, ph)
                        if u == 3 and with_prev:
                            weigh_y(pe_, ph)
                    with dve.Fori(1, 3) as g:
                        for u in range(4):
                            round_(4 * g + u, u)
                    for u in range(4):
                        m = 12 + u
                        if not tail:
                            for t in TOK_AT.get(m, ()):
                                split_tok(i + 1, 1 - half, t)
                        round_(m, u, not tail or m + 3 < MC)

            experts(dve, expert)
            read_y(E - 1, 1)
            scale_y(E - 1, 1)
            weigh_y(E - 1, 1)

        @block.scalar
        def _(act):
            def step(s, r):
                q, q1 = r % 2, (r + 1) % 2
                if live(s):
                    act.wait_ge(nq_ok, s + 1)
                    act.wait_ge(kb_mm, s + 1)
                    act.activation(uv[:, 0, :], KB[:, :], ACT.Relu, bias=nq[:, 0:1], scale=-1.0)
                    act.activation(uv[:, 1, :], KB[:, :], ACT.Relu, bias=qm[:, 0:1]).then_inc(uv_ok, 1)
                    wait(act, att_ok, KC * s)
                    act.activation(fA[:, q, :], qs[:, q, :], ACT.Exp, bias=nq[:, 0:1])
                    act.activation(fC[:, q, :], qs[:, q, :], ACT.Exp, bias=nq[:, 1:2], scale=SLOPE)
                    act.wait_ge(uv_ok, s + 1)
                    act.activation(fB[:, q, :], uv[:, 0, :], ACT.Exp, scale=SLOPE - 1.0)
                    act.activation(fD[:, q, :], uv[:, 1, :], ACT.Exp, scale=SLOPE - 1.0).then_inc(fac_ok, 1)
                if live(s - 3):
                    b = s - 3
                    act.wait_ge(ra_ok, b + 1)
                    wait(act, s_ra2, 7 * b)
                    for j in range(CT):
                        ins = act.activation(ex[:, j, :], m8[:, j, :], ACT.Exp, bias=nm[:, j:j + 1],
                                             accum_out=Z[:, j:j + 1])
                    ins.then_inc(ex_ok, 1)
                if live(s - 2):
                    b = s - 2
                    wait(act, lg_mm, b)
                    for j in range(CT):
                        act.wait_ge(t_mm, CT * b + (j + 1))
                        act.activation(xT[:, j, :, :].rearrange("p k t -> p (k t)"), TP[j][:, :], ACT.Copy)\
                            .then_inc(xT_ok, 1)
                if live(s):
                    act.wait_ge(y_mm, s + 1)
                    wait(act, ag_mm, s - 1)
                    for h in range(2):
                        ins = act.activation(yT[:, q, 2 * h:2 * h + 2, :].rearrange("p k c -> p (k c)"),
                                             Y[h][:, :], ACT.Copy)
                    ins.then_inc(yT_ok, 1)
                    act.wait_ge(fac_ok, s + 1)
                    for k in range(KC):
                        act.activation(tq[:, k, :], fB[:, q, :], ACT.Copy, scale=fA[:, q, k:k + 1])\
                            .then_inc(tq_ok, 1)
                if live(s - 1):
                    for c in range(CT):
                        act.wait_ge(z_ok, CT * (s - 1) + (c + 1))
                        act.activation(z[:, c, :], z[:, c, :], ACT.Relu, bias=bm_sb[:, c:c + 1]).then_inc(relu_ok, 1)

            act.wait_ge(ld_const, 16 * 8)
            act.wait_ge(st_empty, 32)
            act.wait_ge(c_pool, INIT_OPS)
            steps(act, step)

            def split_w(M, sl, par):
                act.wait_ge(ld_w[par], 8 * (M - par) + 16)
                wait(act, fc2_mm, M - 3)
                act.activation(w_hi[:, sl, :], w_raw[:, par, :], ACT.Copy).then_inc(w_hi_ok, 1)

            def gelu(M, e, m):
                for n in range(2):
                    wait(act, h_ready, 2 * M + (n - 1))
                    wait_apart(act, apart, fc1_mm, 2 * M + (n + 1))
                    act.activation(h_raw[:, n, :], HB[n][:, 0:NH], ACT.Gelu, bias=b1_sb[:, bass.ds(16 * e + m, 1)])\
                        .then_inc(gelu_ok, 1)

            for M in range(3):
                split_w(M, M % RING_W, M % 2)

            def expert(e, first, last):
                for half in range(2):
                    i = 2 * e + half
                    tail = last and half == 1
                    for u in range(4):
                        gelu(16 * i + u, e, u)
                        split_w(16 * i + (u + 3), (u + 3) % RING_W, (u + 3) % 2)
                    with act.Fori(1, 3) as g:
                        for u in range(4):
                            gelu(16 * i + 4 * g + u, e, 4 * g + u)
                            split_w(16 * i + 4 * g + (u + 3), (u + 3) % RING_W, (u + 3) % 2)
                    for u in range(4):
                        m = 12 + u
                        gelu(16 * i + m, e, m)
                        if not tail or m + 3 < MC:
                            split_w(16 * i + (m + 3), (u + 3) % RING_W, (u + 3) % 2)

            experts(act, expert)

        @block.tensor
        def _(pe):
            pe.wait_ge(ld_const, 16 * 8)
            pe.wait_ge(c_pool, INIT_OPS)
            pe.wait_ge(c_dve, CT)

            def step(s, r):
                q, q1 = r % 2, (r + 1) % 2
                if live(s):
                    pe.wait_ge(xn_ok, s + 1)
                    if isinstance(s, int) and s < 2:
                        wait(pe, uv_ok, s)
                    wait(pe, rden_ok, s - 1)
                    for c in range(CT):
                        ins = pe.matmul(KB[:, :], wk_rep[:, c, :], xn[:, q, c, :], start=(c == 0), stop=(c == CT - 1))
                    ins.then_inc(kb_mm, 1)
                    wait(pe, lg_read, s - 3 + 1)
                    wait(pe, rank_read, s - 4 + 1)
                    for k in range(KC):
                        for c in range(CT):
                            ins = pe.matmul(q_ps[:, k:k + 1], xn[:, q, c, k * P:(k + 1) * P], wq_sb[:, c:c + 1],
                                            start=(c == 0), stop=(c == CT - 1))
                    ins.then_inc(q_mm, 1)
                    wait(pe, yT_ok, s)
                    for k in range(KC):
                        for c in range(CT):
                            ins = pe.matmul(Y[k // 2][:, (k % 2) * C:(k % 2 + 1) * C], xn[:, q, c, k * P:(k + 1) * P],
                                            adj_sb[:, c, :], start=(c == 0), stop=(c == CT - 1))
                    ins.then_inc(y_mm, 1)
                def aggregate(b, ks):
                    for k in ks:
                        pe.wait_ge(att_ok, KC * b + (k + 1))
                        for c in range(CT):
                            ins = pe.matmul(AG[c][:, :], yT[:, q1, k, c * P:(c + 1) * P], att[:, k, :],
                                            start=(k == 0), stop=(k == KC - 1))
                    return ins

                if live(s - 1):
                    b = s - 1
                    pe.wait_ge(yT_ok, b + 1)
                    wait(pe, z_ok, CT * b)
                    aggregate(b, (0, 1))
                    pe.wait_ge(asum_ok, b + 1)
                    if live(s):
                        pe.wait_ge(uv_ok, s + 1)
                    pe.matmul(DEN[:, :], ones[:, :], asum[:, :], start=True, stop=True).then_inc(den_mm, 1)
                if live(s - 2):
                    b = s - 2
                    pe.wait_ge(xn2_ok, b + 1)
                    for j in range(CT):
                        wait(pe, xT_ok, CT * (b - 1) + j + 1)
                        for k in range(KC):
                            ins = pe.transpose(TP[j][:, k * P:(k + 1) * P], xn2[:, j, k * P:(k + 1) * P], ident[:, :])
                        ins.then_inc(t_mm, 1)
                if live(s - 1):
                    aggregate(s - 1, (2, 3)).then_inc(ag_mm, 1)
                if live(s):
                    pe.wait_ge(q_read, s + 1)
                if live(s - 3):
                    b = s - 3
                    pe.wait_ge(oh_ok, b + 1)
                    if not live(s):
                        wait(pe, lg_read, b + 1)
                        wait(pe, rank_read, b)
                    pe.matmul(rank_ps, lower[:, :], onehot[:, :, :].rearrange("p j e -> p (j e)"),
                              start=True, stop=False)
                    pe.matmul(rank_ps, ones[:, :], seen[:, q1, :, :].rearrange("p j e -> p (j e)"),
                              start=False, stop=True).then_inc(rank_mm, 1)
                if live(s - 2):
                    b = s - 2
                    for j in range(CT):
                        pe.wait_ge(xT_ok, CT * b + (j + 1))
                        for k in range(KC):
                            ins = pe.matmul(lg_ps[:, j, :], xT[:, j, k, :], rw_sb[:, k, :], start=(k == 0),
                                            stop=(k == KC - 1))
                    ins.then_inc(lg_mm, 1)

            steps(pe, step)
            pe.wait_ge(rank_read, B)
            pe.matmul(cnt_ps, ones[:, :], seen[:, B % 2, 0, 0:E], start=True, stop=True).then_inc(cnt_mm, 1)

            def tok_transpose(i, e, half, t, to=TB):
                pe.wait_ge(ga[half], 16 * TT * (e + 1))
                if to is TB:
                    wait(pe, tok_ready, TT * i + t)
                for k in range(KC):
                    ins = pe.transpose(to[:, k * TM:(k + 1) * TM], rows[0:TM, half, t, k * P:(k + 1) * P],
                                       ident[0:TM, 0:TM])
                ins.then_inc(tok_mm, 1)

            def fc1(i, M, half, sl):
                pe.wait_ge(w_ready, M + 1)
                for n in range(2):
                    wait(pe, gelu_ok, 2 * M + (n - 1))
                    cols = slice(n * NH, (n + 1) * NH)
                    for k in range(KC):
                        wk_ = slice(k * P, (k + 1) * P)
                        for a, t in ((w_hi, t_hi), (w_hi, t_lo), (w_lo, t_hi)):
                            ins = pe.matmul(HB[n][:, 0:NH], a[:, sl, wk_], t[:, half, k, cols],
                                            start=(k == 0 and a is w_hi and t is t_hi),
                                            stop=(k == KC - 1 and a is w_lo))
                    ins.then_inc(fc1_mm, 1)

            def fc2(M, sl, par, start, stop, read=None):
                pe.wait_ge(h_ready, 2 * M + 2)
                for t in range(TT):
                    if read is not None:
                        pe.wait_ge(y_read, read + (t + 1))
                    cols = slice(t * TM, (t + 1) * TM)
                    for a, w in ((h_hi, w_hi), (h_hi, w_lo), (h_lo, w_hi)):
                        ins = pe.matmul(YB[t][0:TM, :], a[:, par, cols], w[:, sl, N:2 * N],
                                        start=(start and a is h_hi and w is w_hi), stop=(stop and a is h_lo))
                ins.then_inc(fc2_mm, 1)

            pe.wait_ge(cnt_ok, 1)
            for t in range(TT):
                tok_transpose(0, 0, 0, t, YB[t])

            def expert(e, first, last):
                for half in range(2):
                    i = 2 * e + half
                    tail = last and half == 1
                    ne, nh = (e + 1, 0) if half else (e, 1)
                    for u in range(4):
                        if u == 0:
                            pe.wait_ge(tok_ready, TT * i + TT)
                        fc1(i, 16 * i + u, half, u)
                        if u == 0 and not (first and half == 0):
                            fc2(16 * i - 1, 3, 1, False, True)
                        if u > 0:
                            fc2(16 * i + (u - 1), u - 1, (u - 1) % 2, u == 1, False,
                                read=TT * (i - 1) if u == 1 and not (first and half == 0) else None)
                    with pe.Fori(1, 3) as g:
                        for u in range(4):
                            fc1(i, 16 * i + 4 * g + u, half, u)
                            fc2(16 * i + 4 * g + (u - 1), (u - 1) % 4, (u - 1) % 2, False, False)
                    for u in range(4):
                        m = 12 + u
                        todo = () if tail else TOK_AT.get(m, ())
                        for t in todo[0:1]:
                            tok_transpose(i + 1, ne, nh, t)
                        fc1(i, 16 * i + m, half, u)
                        for t in todo[1:2]:
                            tok_transpose(i + 1, ne, nh, t)
                        fc2(16 * i + (m - 1), (u - 1) % 4, (u - 1) % 2, False, False)

            experts(pe, expert)
            fc2(16 * PASSES - 1, 3, 1, False, True)


TOK_AT = {12: (0, 1), 13: (2, 3), 14: (4,)}


def kernel(**inputs):
    import numpy as np
    import concourse.bacc as bacc
    from concourse.bass_utils import run_bass_kernel_spmd

    g = {k: np.asarray(v) for k, v in inputs.items()}
    fc1 = g["L0_ffn_fc1_w"].reshape(E, MC, P, KC, P).transpose(0, 1, 4, 3, 2).reshape(E, MC, P, N)
    fc2 = g["L0_ffn_fc2_w"].reshape(E, N, MC, P).transpose(0, 2, 3, 1)
    arrays = {
        "x": g["x"],
        "adj_t": g["adj"].T,
        "wq": g["L0_gnn_wq"],
        "wk": g["L0_gnn_wk"],
        "bm": g["L0_gnn_bm"],
        "router_wt": g["L0_ffn_router_w"].T,
        "router_b": g["L0_ffn_router_b"],
        "w_cat": np.concatenate([fc1, fc2], axis=3),
        "fc1_b": g["L0_ffn_fc1_b"].reshape(E * MC, P).T,
        "fc2_b": g["L0_ffn_fc2_b"],
        "scale": g["L0_ffn_layer_scale"],
    }
    nc = bacc.Bacc("TRN2", target_bir_lowering=False, num_devices=1)
    arrays = {k: np.ascontiguousarray(v) for k, v in arrays.items()}
    args = [nc.dram_tensor(k, v.shape, F32, kind="ExternalInput").ap() for k, v in arrays.items()]
    out = nc.dram_tensor("out", (B, C, N), F32, kind="ExternalOutput").ap()
    gnn_moe_kernel(nc, *args, out)
    r = run_bass_kernel_spmd(nc, [arrays], core_ids=[0])
    return r.results[0]["out"]
```
